# Optimizing a Trainium2 kernel written in Bass

```python
import numpy as np
import jax
import jax.numpy as jnp

def _softmax(x, axis=-1):
    return jax.nn.softmax(x, axis=axis)

def _gelu(x):
    return jax.nn.gelu(x, approximate=True)

def _silu(x):
    return jax.nn.silu(x)

def _sigmoid(x):
    return jax.nn.sigmoid(x)

def _layernorm(x, axis=-1, eps=1e-05):
    m = jnp.mean(x, axis=axis, keepdims=True)
    v = jnp.var(x, axis=axis, keepdims=True)
    return (x - m) / jnp.sqrt(v + eps)

def _scatter_add(tgt, idx, src, axis=0):
    return tgt.at[idx].add(src)

def _segment_sum(src, seg, n):
    return jax.ops.segment_sum(src, seg, n)
kernel_name = 'mk_cond_seq_d1_seqx_r8_09b598'

def setup_inputs(seed: int=0):
    np.random.seed(seed)
    _w = jnp.asarray

    def _rec_inputs():
        import jax
        import jax.numpy as jnp
        _rk = jax.random.key(seed)
        x = -0.0002928 + 1 * jax.random.normal(jax.random.fold_in(_rk, 1), (128, 32, 128), jnp.float32)
        _lenS = 32 - jax.random.randint(jax.random.fold_in(_rk, 7), (128,), 0, max(1, 32 // 4) + 1, jnp.int32)
        _lenS2 = 32 - jax.random.randint(jax.random.fold_in(_rk, 8), (128,), 0, max(1, 32 // 4) + 1, jnp.int32)
        itok_B_6_14 = jax.random.randint(jax.random.fold_in(_rk, 11), (128,), 6, 15, jnp.int32)
        return (x, itok_B_6_14)
    x, itok_B_6_14 = _rec_inputs()

    def _L0_cond_setup():
        import jax, jax.numpy as jnp
        import numpy as np
        D = 128
        E = 8
        FF = 512
        TOPK = 2
        S = 32
        SE = 64
        SH = 128
        B, T = (2, 256)

        def _forward(x, subject_ids, ln_g, ln_b, subj_emb, hyp_w1, hyp_b1, hyp_w2, hyp_b2, sty_w1, sty_b1, sty_w2, sty_b2, router_w, exp_w1, exp_b1, exp_w2, exp_b2):
            mu = x.mean(-1, keepdims=True)
            var = x.var(-1, keepdims=True)
            h = (x - mu) * jax.lax.rsqrt(var + 1e-05) * ln_g + ln_b
            m_t = h.mean(1, keepdims=True)
            v_t = h.var(1, keepdims=True)
            h_norm = (h - m_t) * jax.lax.rsqrt(v_t + 1e-08)
            se = subj_emb[subject_ids]
            hyp = jax.nn.relu(se @ hyp_w1 + hyp_b1) @ hyp_w2 + hyp_b2
            sty = jax.nn.relu(hyp @ sty_w1 + sty_b1) @ sty_w2 + sty_b2
            gamma, beta = jnp.split(sty, 2, axis=-1)
            gamma = jax.nn.softplus(gamma) + 1e-08
            h = h_norm * gamma[:, None, :] + beta[:, None, :]
            h_flat = h.reshape(-1, D)
            probs = jax.nn.softmax(h_flat @ router_w, axis=-1)
            gates, idx = jax.lax.top_k(probs, TOPK)
            gates = gates / gates.sum(-1, keepdims=True)
            N = h_flat.shape[0]
            combine = jnp.zeros((N, E), h_flat.dtype).at[jnp.arange(N)[:, None], idx].add(gates)
            hid = jax.nn.relu(jnp.einsum('nd,edf->nef', h_flat, exp_w1) + exp_b1)
            eout = jnp.einsum('nef,efd->ned', hid, exp_w2) + exp_b2
            y = jnp.einsum('ned,ne->nd', eout, combine)
            return x + y.reshape(x.shape)
        key = jax.random.key(seed)
        ks = jax.random.split(key, 16)
        n = lambda k, sh, s=0.02: jax.random.normal(k, sh, dtype=jnp.float32) * s
        return {'x': jax.random.normal(ks[0], (B, T, D), dtype=jnp.float32), 'subject_ids': jax.random.randint(ks[1], (B,), 0, S), 'ln_g': jnp.ones((D,), jnp.float32), 'ln_b': jnp.zeros((D,), jnp.float32), 'subj_emb': n(ks[2], (S, SE)), 'hyp_w1': n(ks[3], (SE, SH), 1.0 / np.sqrt(SE)), 'hyp_b1': jnp.zeros((SH,), jnp.float32), 'hyp_w2': n(ks[4], (SH, SH), 1.0 / np.sqrt(SH)), 'hyp_b2': jnp.zeros((SH,), jnp.float32), 'sty_w1': n(ks[5], (SH, SH // 2), 1.0 / np.sqrt(SH)), 'sty_b1': jnp.zeros((SH // 2,), jnp.float32), 'sty_w2': n(ks[6], (SH // 2, 2 * D), 1.0 / np.sqrt(SH // 2)), 'sty_b2': jnp.zeros((2 * D,), jnp.float32), 'router_w': n(ks[7], (D, E), 1.0 / np.sqrt(D)), 'exp_w1': n(ks[8], (E, D, FF), 1.0 / np.sqrt(D)), 'exp_b1': jnp.zeros((E, FF), jnp.float32), 'exp_w2': n(ks[9], (E, FF, D), 1.0 / np.sqrt(FF)), 'exp_b2': jnp.zeros((E, D), jnp.float32)}
    _L0_cond_all = _L0_cond_setup()
    _L0_cond_in = {k: v for k, v in _L0_cond_all.items() if k in ('ln_g', 'ln_b', 'subj_emb', 'hyp_w1', 'hyp_b1', 'hyp_w2', 'hyp_b2', 'sty_w1', 'sty_b1', 'sty_w2', 'sty_b2', 'router_w', 'exp_w1', 'exp_b1', 'exp_w2', 'exp_b2')}
    del _L0_cond_all
    return {'x': x, 'itok_B_6_14': itok_B_6_14, 'L0_cond_ln_g': _L0_cond_in['ln_g'], 'L0_cond_ln_b': _L0_cond_in['ln_b'], 'L0_cond_subj_emb': _L0_cond_in['subj_emb'], 'L0_cond_hyp_w1': _L0_cond_in['hyp_w1'], 'L0_cond_hyp_b1': _L0_cond_in['hyp_b1'], 'L0_cond_hyp_w2': _L0_cond_in['hyp_w2'], 'L0_cond_hyp_b2': _L0_cond_in['hyp_b2'], 'L0_cond_sty_w1': _L0_cond_in['sty_w1'], 'L0_cond_sty_b1': _L0_cond_in['sty_b1'], 'L0_cond_sty_w2': _L0_cond_in['sty_w2'], 'L0_cond_sty_b2': _L0_cond_in['sty_b2'], 'L0_cond_router_w': _L0_cond_in['router_w'], 'L0_cond_exp_w1': _L0_cond_in['exp_w1'], 'L0_cond_exp_b1': _L0_cond_in['exp_b1'], 'L0_cond_exp_w2': _L0_cond_in['exp_w2'], 'L0_cond_exp_b2': _L0_cond_in['exp_b2']}

def reference(x, itok_B_6_14, L0_cond_ln_g, L0_cond_ln_b, L0_cond_subj_emb, L0_cond_hyp_w1, L0_cond_hyp_b1, L0_cond_hyp_w2, L0_cond_hyp_b2, L0_cond_sty_w1, L0_cond_sty_b1, L0_cond_sty_w2, L0_cond_sty_b2, L0_cond_router_w, L0_cond_exp_w1, L0_cond_exp_b1, L0_cond_exp_w2, L0_cond_exp_b2):
    import jax
    import jax.numpy as jnp

    def _L0_cond_ref(x, subject_ids, ln_g, ln_b, subj_emb, hyp_w1, hyp_b1, hyp_w2, hyp_b2, sty_w1, sty_b1, sty_w2, sty_b2, router_w, exp_w1, exp_b1, exp_w2, exp_b2):
        import jax, jax.numpy as jnp
        import numpy as np
        D = 128
        E = 8
        FF = 512
        TOPK = 2
        S = 32
        SE = 64
        SH = 128
        B, T = (2, 256)

        def _forward(x, subject_ids, ln_g, ln_b, subj_emb, hyp_w1, hyp_b1, hyp_w2, hyp_b2, sty_w1, sty_b1, sty_w2, sty_b2, router_w, exp_w1, exp_b1, exp_w2, exp_b2):
            mu = x.mean(-1, keepdims=True)
            var = x.var(-1, keepdims=True)
            h = (x - mu) * jax.lax.rsqrt(var + 1e-05) * ln_g + ln_b
            m_t = h.mean(1, keepdims=True)
            v_t = h.var(1, keepdims=True)
            h_norm = (h - m_t) * jax.lax.rsqrt(v_t + 1e-08)
            se = subj_emb[subject_ids]
            hyp = jax.nn.relu(se @ hyp_w1 + hyp_b1) @ hyp_w2 + hyp_b2
            sty = jax.nn.relu(hyp @ sty_w1 + sty_b1) @ sty_w2 + sty_b2
            gamma, beta = jnp.split(sty, 2, axis=-1)
            gamma = jax.nn.softplus(gamma) + 1e-08
            h = h_norm * gamma[:, None, :] + beta[:, None, :]
            h_flat = h.reshape(-1, D)
            probs = jax.nn.softmax(h_flat @ router_w, axis=-1)
            gates, idx = jax.lax.top_k(probs, TOPK)
            gates = gates / gates.sum(-1, keepdims=True)
            N = h_flat.shape[0]
            combine = jnp.zeros((N, E), h_flat.dtype).at[jnp.arange(N)[:, None], idx].add(gates)
            hid = jax.nn.relu(jnp.einsum('nd,edf->nef', h_flat, exp_w1) + exp_b1)
            eout = jnp.einsum('nef,efd->ned', hid, exp_w2) + exp_b2
            y = jnp.einsum('ned,ne->nd', eout, combine)
            return x + y.reshape(x.shape)
        return _forward(x, subject_ids, ln_g, ln_b, subj_emb, hyp_w1, hyp_b1, hyp_w2, hyp_b2, sty_w1, sty_b1, sty_w2, sty_b2, router_w, exp_w1, exp_b1, exp_w2, exp_b2)
    x = _L0_cond_ref(x, itok_B_6_14, L0_cond_ln_g, L0_cond_ln_b, L0_cond_subj_emb, L0_cond_hyp_w1, L0_cond_hyp_b1, L0_cond_hyp_w2, L0_cond_hyp_b2, L0_cond_sty_w1, L0_cond_sty_b1, L0_cond_sty_w2, L0_cond_sty_b2, L0_cond_router_w, L0_cond_exp_w1, L0_cond_exp_b1, L0_cond_exp_w2, L0_cond_exp_b2)
    return x

_drawn_inputs = setup_inputs


def setup_inputs(seed=0):
    import zlib

    import numpy as np

    out = dict(_drawn_inputs(seed))
    spreads = {'L0_cond_ln_g': (1.0, 0.2),
     'L0_cond_ln_b': (0.0, 0.1),
     'L0_cond_hyp_b1': (0.0, 0.1),
     'L0_cond_hyp_b2': (0.0, 0.1),
     'L0_cond_sty_b1': (0.0, 0.1),
     'L0_cond_sty_b2': (0.0, 0.1),
     'L0_cond_exp_b1': (0.0, 0.1),
     'L0_cond_exp_b2': (0.0, 0.1)}
    factors = {}
    for name, (base, spread) in spreads.items():
        noise = np.random.default_rng([zlib.crc32(name.encode()), seed]).standard_normal(out[name].shape)
        drawn = base * np.exp(spread * noise) if base else spread * noise
        out[name] = jnp.asarray(drawn.astype(out[name].dtype))
    for name, factor in factors.items():
        out[name] = (out[name] * factor).astype(out[name].dtype)
    return out
```

```python
import concourse.bass as bass
from concourse import mybir
from contextlib import ExitStack

B, T, D = 128, 32, 128
E, FF = 8, 512
SE, SH, S2 = 64, 128, 64
P = 128
FC = FF // P
TOPK = 2
GROUPS = 2
TG = T // GROUPS
CHUNK = 8
NCH = T // CHUNK
ROW = D + 2
MIN_TILES = TOPK * TG * B // P
TILES = MIN_TILES + E - 1
NT = GROUPS * TILES
REGION = TG * B + P
GROUP_ROWS = E * REGION + (E - 1) * P
NOWHERE = 1 << 20
RING = 8
EPS_LN, EPS_IN, EPS_SP = 1e-5, 1e-8, 1e-8
BIG = 1e30


def later(i, n):
    return i >= n if isinstance(i, int) else True


def each_tile(eng, n_tiles, whole, step):
    for k in range(min(RING, n_tiles)):
        step(0, k)
    if whole > 1:
        with eng.Fori(1, whole, 1) as turn:
            for k in range(RING):
                step(turn, k)
    for i in range(max(whole, 1) * RING, n_tiles):
        step(i // RING, i % RING)


def conditional_moe_kernel(nc, x, ids, ln_g, ln_b, subj_emb, hyp_w1, hyp_b1, hyp_w2, hyp_b2,
                           sty_w1, sty_b1, sty_w2, sty_b2, router_w, exp_w1, exp_b1, exp_w2, exp_b2, out):
    fp32, f32r, i32 = mybir.dt.float32, mybir.dt.float32r, mybir.dt.int32
    ALU, ACT, AX = mybir.AluOpType, mybir.ActivationFunctionType, mybir.AxisListType

    ctx = ExitStack()
    with ctx:
        def sb(name, shape, dt=fp32):
            return ctx.enter_context(nc.sbuf_tensor(name, shape, dt))

        def sem(name):
            return ctx.enter_context(nc.semaphore(name))

        rows = nc.dram_tensor("rows", [GROUPS * GROUP_ROWS, ROW], fp32, kind="Internal").ap()
        results = nc.dram_tensor("results", [TOPK * B * T, D], fp32, kind="Internal").ap()

        X = sb("X", [P, T, D])
        Z = sb("Z", [P, T, D])
        Q = sb("Q", [P, T, D])
        H = sb("H", [P, T, ROW])
        raw1 = H[:, :, :].rearrange("p t r -> p (t r)")[:, 0:E * FF]
        raw2 = Z[:, :, :].rearrange("p t d -> p (t d)")
        rawb = Q[:, :, :].rearrange("p t d -> p (t d)")
        W1h, W1l, W2h, W2l = (sb(n, [P, E * FF], f32r) for n in ("W1h", "W1l", "W2h", "W2l"))
        BIAS = sb("BIAS", [P, E * FF], f32r)
        pick1 = sb("pick1", [P, P], f32r)
        pick2 = sb("pick2", [P, P], f32r)
        pickf = sb("pickf", [P, 2, P])
        ident = sb("ident", [P, P])
        lower = sb("lower", [P, P])
        ones = sb("ones", [P, 2 * P])
        filling = sb("filling", [P, ROW])
        idx = sb("idx", [P, 1], i32)
        se = sb("se", [P, SE])
        seT = sb("seT", [SE, P])
        hyp1T = sb("hyp1T", [SH, P])
        hyp2T = sb("hyp2T", [SH, P])
        sty1T = sb("sty1T", [S2, P])
        w_hyp1 = sb("w_hyp1", [SE, SH])
        w_hyp2 = sb("w_hyp2", [SH, SH])
        w_sty1 = sb("w_sty1", [SH, S2])
        w_sty2 = sb("w_sty2", [S2, 2 * D])
        b_hyp1 = sb("b_hyp1", [SH, 1])
        b_hyp2 = sb("b_hyp2", [SH, 1])
        b_sty1 = sb("b_sty1", [S2, 1])
        b_sty2 = sb("b_sty2", [1, 2 * D])
        w_router = sb("w_router", [D, E])
        gB = sb("gB", [P, D])
        bB = sb("bB", [P, D])
        stats = sb("stats", [P, T, 6])
        st = sb("st", [P, 5, T])
        gam = sb("gam", [P, 4, D])
        co = sb("co", [P, 10, D])
        mk = sb("mk", [P, TOPK, T * E])
        rt = sb("rt", [P, 6, T * E])
        rs = sb("rs", [P, 8, T])
        gate = sb("gate", [P, TOPK, T])
        tie = sb("tie", [P, E])
        tie_i = sb("tie_i", [P, E], i32)
        both = sb("both", [P, GROUPS * E * TG])
        scan = sb("scan", [P, 1 + GROUPS * E * TG])
        cnt = sb("cnt", [P, 4, GROUPS * E])
        first = sb("first", [P, GROUPS * E])
        first_i = sb("first_i", [P, GROUPS * E], i32)
        place = sb("place", [P, TOPK, T], i32)
        tt = sb("tt", [1, 6, GROUPS * E])
        tt_i = sb("tt_i", [1, 2, GROUPS * E], i32)
        tw = sb("tw", [1, 3, TILES * E])
        at = sb("at", [1, TILES])
        at_i = sb("at_i", [1, TILES], i32)
        tn = sb("tn", [1, 4, TILES])
        row_of = sb("row_of", [1, NT], i32)
        expert_of = sb("expert_of", [1, NT], i32)
        fill_at = sb("fill_at", [1, GROUPS * E], i32)
        tile_in = sb("tile_in", [P, RING, ROW])
        hTh, hTl = sb("hTh", [P, 2, P], f32r), sb("hTl", [P, 2, P], f32r)
        hid = sb("hid", [P, 2, FF])
        gTh, gTl = sb("gTh", [P, 2, FF], f32r), sb("gTl", [P, 2, FF], f32r)
        y = sb("y", [P, 4, D])

        ps = ctx.enter_context(nc.psum_tensor("ps", [P, 8, 512], fp32))
        pSeT, pHyp1, pHyp2, pSty1 = ps[0:SE, 0, 0:P], ps[0:SH, 0, P:2 * P], ps[0:SH, 0, 2 * P:3 * P], ps[0:S2, 0, 3 * P:4 * P]
        pSty = ps[:, 1, 0:2 * D]
        pMean, pVar = ps[:, 2, :], ps[:, 3, :]
        pLogit = ps[:, 1, 2 * D:2 * D + T * E]
        pCount = ps[:, 0, 0:2 * GROUPS * E]
        pHT = [ps[:, 4 + n, :] for n in range(4)]
        pHid, pGT = [ps[:, n, :] for n in range(2)], [ps[:, 2 + n, :] for n in range(2)]
        pTile, pY = [ps[:, 4 + n, 0:P] for n in range(2)], [ps[:, 6 + n, 0:D] for n in range(2)]

        x_in = [sem(f"x_in{c}") for c in range(NCH)]
        ids_in, se_in, style_in, norm_in = sem("ids_in"), sem("se_in"), sem("style_in"), sem("norm_in")
        stage_in = [sem(f"stage_in{n}") for n in range(3)]
        consts, bias_zero = sem("consts"), sem("bias_zero")
        pool_step, dve_step, act_step = sem("pool_step"), sem("dve_step"), sem("act_step")
        seT_ps, seT_sb, hyp1_ps, hyp1_sb, hyp2_ps, hyp2_sb, sty1_ps, sty1_sb, sty_ps = (
            sem(n) for n in ("seT_ps", "seT_sb", "hyp1_ps", "hyp1_sb", "hyp2_ps", "hyp2_sb", "sty1_ps", "sty1_sb", "sty_ps"))
        gamma_ln = sem("gamma_ln")
        var_ready, sd_ready, z_ready, mean_ps = sem("var_ready"), sem("sd_ready"), sem("z_ready"), sem("mean_ps")
        zc_ready, sq_ready, var_ps, vt_ready, sdt_ready = (
            sem(n) for n in ("zc_ready", "sq_ready", "var_ps", "vt_ready", "sdt_ready"))
        h_ready, hT_ps, hT_sb, logit_ps = sem("h_ready"), sem("hT_ps"), sem("hT_sb"), sem("logit_ps")
        d_ready, exp_ready, runs_ready, count_ps = sem("d_ready"), sem("exp_ready"), sem("runs_ready"), sem("count_ps")
        place_ready, gate_ready, fill_ready, tiles_ready = (
            sem(n) for n in ("place_ready", "gate_ready", "fill_ready", "tiles_ready"))
        w_hi, w_lo = sem("w_hi"), sem("w_lo")
        sent = [[sem(f"sent{c}_{k}") for k in range(TOPK)] for c in range(NCH)]
        filled = [sem(f"filled{g}") for g in range(GROUPS)]
        loaded = [sem(f"loaded{n}") for n in range(RING)]
        returned = [sem(f"returned{n}") for n in range(4)]
        to_return = sem("to_return")
        tile_ps, tile_hi, tile_lo = sem("tile_ps"), sem("tile_hi"), sem("tile_lo")
        hid_ps, hid_sb, g_ps, g_hi, g_lo, y_ps, y_sb = (
            sem(n) for n in ("hid_ps", "hid_sb", "g_ps", "g_hi", "g_lo", "y_ps", "y_sb"))
        back_in = [[sem(f"back{c}_{k}") for k in range(TOPK)] for c in range(NCH)]
        out_ready, out_done = sem("out_ready"), sem("out_done")

        block = ctx.enter_context(nc.Block())

        def times_returned(turn, k):
            return 16 * (2 * turn + k // 4 + 1)

        @block.sync
        def _(sp):
            for c in range(NCH):
                sp.dma_start(X[:, c * CHUNK:(c + 1) * CHUNK, :], x[:, c * CHUNK:(c + 1) * CHUNK, :]).then_inc(x_in[c], 16)
            sp.dma_start(raw1.rearrange("d (e f) -> d e f", e=E), exp_w1.rearrange("e d f -> d e f")).then_inc(stage_in[0], 16)
            sp.wait_ge(h_ready, T // 4)
            sp.dma_start(raw2.rearrange("p (n d) -> p n d", d=D),
                         exp_w2.rearrange("e (c p) d -> p (e c) d", p=P)).then_inc(stage_in[1], 16)

            sp.wait_ge(consts, 1)
            sp.wait_ge(fill_ready, 1)
            for g in range(GROUPS):
                for n in range(E - 1):
                    r = g * GROUP_ROWS + E * REGION + n * P
                    sp.dma_start(rows[r:r + P, :], filling[:, :]).then_inc(filled[g], 16)
                for e in range(E):
                    j = g * E + e
                    r = sp.value_load(fill_at[0:1, j:j + 1], min_val=0, max_val=GROUPS * GROUP_ROWS - P)
                    sp.dma_start(rows[bass.ds(r, P), :], filling[:, :]).then_inc(filled[g], 16)

            sp.wait_ge(bias_zero, 1)
            for r in (0, 32):
                sp.dma_start(rawb[r:r + 1, :], exp_b1.rearrange("(a e) f -> a (e f)", a=1)).then_inc(stage_in[2], 16)
            for r in (64, 96):
                sp.dma_start(rawb[r:r + 1, :].rearrange("a (e f) -> a e f", e=E)[:, :, 0:D],
                             exp_b2.rearrange("(a e) d -> a e d", a=1)).then_inc(stage_in[2], 16)

            sp.wait_ge(tiles_ready, 1)

            def load(turn, k):
                i = turn * RING + k
                r = sp.value_load(row_of[0:1, bass.ds(i, 1)], min_val=0, max_val=GROUPS * GROUP_ROWS - P)
                if later(turn, 1):
                    sp.wait_ge(returned[k % 4], times_returned(turn - 1, k))
                sp.dma_start(tile_in[:, k, :], rows[bass.ds(r, P), :]).then_inc(loaded[k], 16)

            def group_written(g):
                for c in range(g * NCH // GROUPS, (g + 1) * NCH // GROUPS):
                    for k in range(TOPK):
                        sp.wait_ge(sent[c][k], 16 * CHUNK)
                sp.wait_ge(filled[g], 16 * (2 * E - 1))

            group_written(0)
            for k in range(RING):
                load(0, k)
            with sp.Fori(1, TILES // RING, 1) as turn:
                for k in range(RING):
                    load(turn, k)
            for i in range(TILES // RING * RING, TILES):
                load(i // RING, i % RING)
            group_written(1)
            whole = -(-TILES // RING)
            for i in range(TILES, whole * RING):
                load(i // RING, i % RING)
            with sp.Fori(whole, NT // RING, 1) as turn:
                for k in range(RING):
                    load(turn, k)
            for i in range(NT // RING * RING, NT):
                load(i // RING, i % RING)

            for n in range(4):
                sp.wait_ge(returned[n], 16 * len(range(n, NT, 4)))
            res = results.rearrange("(k b t) d -> k b t d", k=TOPK, b=B)
            for c in range(NCH):
                t = slice(c * CHUNK, (c + 1) * CHUNK)
                sp.dma_start(Z[:, t, :], res[0][:, t, :]).then_inc(back_in[c][0], 16)
                sp.dma_start(Q[:, t, :], res[1][:, t, :]).then_inc(back_in[c][1], 16)
            for c in range(NCH):
                t = slice(c * CHUNK, (c + 1) * CHUNK)
                sp.wait_ge(out_ready, c + 1)
                sp.dma_start(out[:, t, :], X[:, t, :]).then_inc(out_done, 16)
            sp.wait_ge(out_done, 16 * NCH)

        @block.gpsimd
        def _(pool):
            steps = [0]

            def settle(ins):
                steps[0] += 1
                ins.then_inc(pool_step, 1)
                pool.wait_ge(pool_step, steps[0])

            pool.wait_ge(ids_in, 16)
            pool.indirect_dma_start(out=se[:, :], out_offset=None, in_=subj_emb[:, :],
                                    in_offset=bass.IndirectOffsetOnAxis(ap=idx[:, 0:1], axis=0)).then_inc(se_in, 16)
            pool.memset(ident[:, :], 0.0)
            pool.memset(lower[:, :], 1.0)
            pool.memset(ones[:, :], 1.0)
            pool.memset(scan[:, 0:1], 0.0)
            pool.memset(pickf[:, :, :], 0.0)
            settle(pool.memset(filling[:, :], 0.0))
            for r in (0, 32):
                settle(pool.memset(pickf[r:r + 1, 0, :], 1.0))
            for r in (64, 96):
                settle(pool.memset(pickf[r:r + 1, 1, :], 1.0))
            pool.iota(filling[:, D + 1:D + 2].bitcast(i32), [[0, 1]], base=NOWHERE, channel_multiplier=0)
            pool.affine_select(out=ident[:, :], in_=ident[:, :], compare_op=ALU.not_equal, fill=1.0,
                               base=0, pattern=[[-1, P]], channel_multiplier=1)
            pool.affine_select(out=lower[:, :], in_=lower[:, :], compare_op=ALU.is_gt, fill=0.0,
                               base=0, pattern=[[1, P]], channel_multiplier=-1)
            pool.iota(at_i[:, :], [[P, TILES]], base=0, channel_multiplier=0)
            pool.iota(first_i[:, :], [[GROUP_ROWS, GROUPS], [REGION, E]], base=-1, channel_multiplier=0)
            settle(pool.iota(tie_i[:, :], [[-1, E]], base=E, channel_multiplier=0))
            pool.tensor_copy(at[:, :], at_i[:, :])
            pool.tensor_copy(first[:, :], first_i[:, :])
            pool.tensor_copy(pick1[:, :], pickf[:, 0, :])
            pool.tensor_copy(pick2[:, :], pickf[:, 1, :])
            pool.tensor_copy(tie[:, :], tie_i[:, :]).then_inc(consts, 1)

            pool.wait_ge(w_hi, 1)
            pool.tensor_tensor(W1l[:, :], raw1, W1h[:, :].bitcast(fp32), ALU.subtract).then_inc(w_lo, 1)
            pool.wait_ge(w_lo, 1)
            settle(pool.iota(H[:, :, D + 1:D + 2].bitcast(i32), [[1, T], [0, 1]], base=0, channel_multiplier=T))

            def send(c, k):
                for t in range(c * CHUNK, (c + 1) * CHUNK):
                    pool.indirect_dma_start(out=rows[:, :], out_offset=bass.IndirectOffsetOnAxis(ap=place[:, k, t:t + 1], axis=0),
                                            in_=H[:, t, :], in_offset=None).then_inc(sent[c][k], 16)

            def turn_over(c):
                pool.wait_ge(sent[c][0], 16 * CHUNK)
                t = slice(c * CHUNK, (c + 1) * CHUNK)
                pool.iota(H[:, t, D + 1:D + 2].bitcast(i32), [[1, CHUNK], [0, 1]], base=B * T + c * CHUNK, channel_multiplier=T)
                settle(pool.tensor_copy(H[:, t, D:D + 1], gate[:, 1, t].rearrange("p (t a) -> p t a", a=1)))

            def give_back(turn, k):
                i = turn * RING + k
                pool.wait_ge(y_sb, i + 1)
                pool.sem_inc(to_return, 1)
                pool.indirect_dma_start(out=results[:, :],
                                        out_offset=bass.IndirectOffsetOnAxis(ap=tile_in[:, k, D + 1:D + 2].bitcast(i32), axis=0),
                                        in_=y[:, k % 4, :], in_offset=None,
                                        bounds_check=limit, oob_is_err=False).then_inc(returned[k % 4], 16)

            pool.wait_ge(h_ready, T // 4)
            pool.wait_ge(place_ready, 2)
            pool.wait_ge(gate_ready, 1)
            per = NCH // GROUPS
            for g in range(GROUPS):
                for c in range(g * per, (g + 1) * per):
                    send(c, 0)
                for c in range(g * per, (g + 1) * per):
                    turn_over(c)
                    send(c, 1)
            limit = pool.to_reg(TOPK * B * T - 1)
            each_tile(pool, NT, NT // RING, give_back)

        @block.scalar
        def _(act):
            act.dma_start(idx[:, :], ids.rearrange("(b a) -> b a", a=1)).then_inc(ids_in, 16)
            act.dma_start(w_hyp1[:, :], hyp_w1).then_inc(style_in, 16)
            act.dma_start(w_hyp2[:, :], hyp_w2).then_inc(style_in, 16)
            act.dma_start(w_sty1[:, :], sty_w1).then_inc(style_in, 16)
            act.dma_start(w_sty2[:, :], sty_w2).then_inc(style_in, 16)
            act.dma_start(b_hyp1[:, :], hyp_b1.rearrange("(b a) -> b a", a=1)).then_inc(style_in, 16)
            act.dma_start(b_hyp2[:, :], hyp_b2.rearrange("(b a) -> b a", a=1)).then_inc(style_in, 16)
            act.dma_start(b_sty1[:, :], sty_b1.rearrange("(b a) -> b a", a=1)).then_inc(style_in, 16)
            act.dma_start(b_sty2[:, :], sty_b2.rearrange("(a b) -> a b", a=1)).then_inc(style_in, 16)
            act.dma_start(w_router[:, :], router_w).then_inc(norm_in, 16)
            act.dma_start(gB[:, :], ln_g.rearrange("(a b) -> a b", a=1).to_broadcast([P, D])).then_inc(norm_in, 16)
            act.dma_start(bB[:, :], ln_b.rearrange("(a b) -> a b", a=1).to_broadcast([P, D])).then_inc(norm_in, 16)

            act.wait_ge(style_in, 16 * 8)
            act.wait_ge(hyp1_ps, 1)
            act.activation(hyp1T[:, :], pHyp1, ACT.Relu, bias=b_hyp1[:, :]).then_inc(hyp1_sb, 1)
            act.wait_ge(hyp2_ps, 1)
            act.activation(hyp2T[:, :], pHyp2, ACT.Identity, bias=b_hyp2[:, :]).then_inc(hyp2_sb, 1)
            act.wait_ge(sty1_ps, 1)
            act.activation(sty1T[:, :], pSty1, ACT.Relu, bias=b_sty1[:, :]).then_inc(sty1_sb, 1)
            act.wait_ge(sty_ps, 1)
            act.activation(gam[:, 0, :], pSty[:, 0:D], ACT.Abs).then_inc(act_step, 1)
            act.wait_ge(act_step, 1)
            act.activation(gam[:, 1, :], gam[:, 0, :], ACT.Exp, scale=-1.0).then_inc(act_step, 1)
            act.wait_ge(act_step, 2)
            act.activation(gam[:, 2, :], gam[:, 1, :], ACT.Ln, bias=1.0).then_inc(gamma_ln, 1)

            for c in range(NCH):
                t = slice(c * CHUNK, (c + 1) * CHUNK)
                act.wait_ge(var_ready, c + 1)
                act.activation(st[:, 2, t], st[:, 1, t], ACT.Sqrt).then_inc(sd_ready, 1)
            act.wait_ge(stage_in[0], 16)
            act.activation(W1h[:, :], raw1, ACT.Copy).then_inc(w_hi, 1)
            for n in range(T // 4):
                act.wait_ge(zc_ready, n + 1)
                act.activation(Q[:, 4 * n:4 * n + 4, :], Q[:, 4 * n:4 * n + 4, :], ACT.Square).then_inc(sq_ready, 1)
            act.wait_ge(vt_ready, 1)
            act.activation(co[:, 3, :], co[:, 2, :], ACT.Sqrt).then_inc(sdt_ready, 1)
            act.wait_ge(var_ps, 1)
            for n in range(T // 4):
                act.wait_ge(hT_ps, n + 1)
                act.activation(Q[:, 4 * n:4 * n + 4, :], pHT[n % 4].rearrange("p (t d) -> p t d", d=P), ACT.Copy).then_inc(hT_sb, 1)
            act.wait_ge(d_ready, 1)
            act.activation(rt[:, 1, :], rt[:, 0, :], ACT.Exp).then_inc(exp_ready, 1)
            act.wait_ge(stage_in[1], 16)
            act.activation(W2h[:, :], raw2, ACT.Copy).then_inc(w_hi, 1)
            act.wait_ge(stage_in[2], 16 * 4)
            act.activation(BIAS[:, :], rawb, ACT.Copy).then_inc(w_hi, 1)

            def step(turn, k):
                i = turn * RING + k
                if later(i, 0) and (not isinstance(i, int) or i < NT):
                    act.wait_ge(tile_ps, i + 1)
                    if later(i, 2):
                        act.wait_ge(hid_ps, i - 1)
                    act.activation(hTh[:, k % 2, :], pTile[k % 2], ACT.Copy).then_inc(tile_hi, 1)
                if later(i, 1) and (not isinstance(i, int) or i - 1 < NT):
                    act.wait_ge(hid_ps, i)
                    if later(i, 3):
                        act.wait_ge(g_ps, i - 2)
                    act.activation(hid[:, (k - 1) % 2, :], pHid[(k - 1) % 2], ACT.Relu).then_inc(hid_sb, 1)
                if later(i, 2) and (not isinstance(i, int) or i - 2 < NT):
                    act.wait_ge(g_ps, i - 1)
                    if later(i, 4):
                        act.wait_ge(y_ps, i - 3)
                    act.activation(gTh[:, k % 2, :], pGT[k % 2], ACT.Copy).then_inc(g_hi, 1)

            each_tile(act, NT + 2, NT // RING, step)

        @block.vector
        def _(dve):
            steps = [0]

            def settle(ins):
                steps[0] += 1
                ins.then_inc(dve_step, 1)
                dve.wait_ge(dve_step, steps[0])

            def over_t(ap, n):
                return ap.rearrange("p (a d) -> p a d", a=1).to_broadcast([P, n, D])

            def over_e(ap):
                return ap.rearrange("p (t a) -> p t a", a=1).to_broadcast([P, T, E])

            V = nc.vector
            MEAN, VAR, SD, RSD, TMP = range(5)

            def layer_stats(c):
                dve.wait_ge(x_in[c], 16)
                for t in range(c * CHUNK, (c + 1) * CHUNK):
                    last = V.bn_stats(stats[:, t, :], X[:, t, :])
                settle(last)
                t = slice(c * CHUNK, (c + 1) * CHUNK)
                me, mo, ve, vo = (stats[:, t, n] for n in (1, 4, 2, 5))
                V.tensor_tensor(st[:, MEAN, t], me, mo, ALU.add)
                V.tensor_tensor(st[:, VAR, t], ve, vo, ALU.add)
                settle(V.tensor_tensor(st[:, TMP, t], me, mo, ALU.subtract))
                V.tensor_scalar(st[:, MEAN, t], st[:, MEAN, t], 0.5, None, ALU.mult)
                V.tensor_scalar(st[:, VAR, t], st[:, VAR, t], 1.0 / D, EPS_LN, ALU.mult, ALU.add)
                settle(V.scalar_tensor_tensor(st[:, TMP, t], st[:, TMP, t], 0.25, st[:, TMP, t], ALU.mult, ALU.mult))
                V.tensor_tensor(st[:, VAR, t], st[:, VAR, t], st[:, TMP, t], ALU.add).then_inc(var_ready, 1)

            def layer_norm(c):
                t = slice(c * CHUNK, (c + 1) * CHUNK)
                dve.wait_ge(sd_ready, c + 1)
                settle(V.reciprocal(st[:, RSD, t], st[:, SD, t]))
                for t in range(c * CHUNK, (c + 1) * CHUNK):
                    last = V.tensor_scalar(Z[:, t, :], X[:, t, :], st[:, MEAN, t:t + 1], st[:, RSD, t:t + 1], ALU.subtract, ALU.mult)
                last.then_inc(z_ready, 1)

            dve.wait_ge(se_in, 16)
            dve.wait_ge(seT_ps, 1)
            V.tensor_copy(seT[:, :], pSeT).then_inc(seT_sb, 1)
            for c in range(NCH + 1):
                if c < NCH:
                    layer_stats(c)
                if c >= 1:
                    layer_norm(c - 1)

            dve.wait_ge(gamma_ln, 1)
            settle(V.scalar_tensor_tensor(gam[:, 3, :], pSty[:, 0:D], 0.0, gam[:, 2, :], ALU.max, ALU.add))
            settle(V.tensor_scalar(gam[:, 3, :], gam[:, 3, :], EPS_SP, None, ALU.add))
            MZ, VZ, VT, SDT, RT, GG, MT, G2, A, C = range(10)
            dve.wait_ge(norm_in, 16 * 3)
            V.tensor_tensor(co[:, G2, :], gB[:, :], gB[:, :], ALU.mult)
            V.tensor_tensor(co[:, GG, :], gB[:, :], gam[:, 3, :], ALU.mult)
            dve.wait_ge(mean_ps, 1)
            settle(V.tensor_reduce(co[:, MZ, :], pMean.rearrange("p (t d) -> p d t", d=D), AX.X, ALU.add))
            settle(V.tensor_scalar(co[:, MZ, :], co[:, MZ, :], 1.0 / T, None, ALU.mult))
            for n in range(T // 4):
                V.tensor_tensor(Q[:, 4 * n:4 * n + 4, :], Z[:, 4 * n:4 * n + 4, :], over_t(co[:, MZ, :], 4), ALU.subtract).then_inc(zc_ready, 1)
            settle(V.tensor_tensor(co[:, MT, :], co[:, MZ, :], gB[:, :], ALU.mult))
            settle(V.tensor_tensor(co[:, MT, :], co[:, MT, :], bB[:, :], ALU.add))
            settle(V.tensor_tensor(co[:, MT, :], bB[:, :], co[:, MT, :], ALU.subtract))
            V.tensor_tensor(co[:, MT, :], co[:, MT, :], gam[:, 3, :], ALU.mult)
            dve.wait_ge(var_ps, 1)
            settle(V.tensor_reduce(co[:, VZ, :], pVar.rearrange("p (t d) -> p d t", d=D), AX.X, ALU.add))
            settle(V.scalar_tensor_tensor(co[:, VT, :], co[:, VZ, :], 1.0 / T, co[:, G2, :], ALU.mult, ALU.mult))
            V.tensor_scalar(co[:, VT, :], co[:, VT, :], EPS_IN, None, ALU.add).then_inc(vt_ready, 1)
            dve.wait_ge(sdt_ready, 1)
            settle(V.reciprocal(co[:, RT, :], co[:, SDT, :]))
            V.tensor_tensor(co[:, A, :], co[:, GG, :], co[:, RT, :], ALU.mult)
            settle(V.tensor_tensor(co[:, C, :], co[:, MT, :], co[:, RT, :], ALU.mult))
            settle(V.tensor_tensor(co[:, C, :], co[:, C, :], pSty[:, D:2 * D], ALU.add))
            dve.wait_ge(w_lo, 1)
            for n in range(T // 4):
                t = slice(4 * n, 4 * n + 4)
                settle(V.tensor_tensor(H[:, t, 0:D], Z[:, t, :], over_t(co[:, A, :], 4), ALU.mult))
                V.tensor_tensor(H[:, t, 0:D], H[:, t, 0:D], over_t(co[:, C, :], 4), ALU.add).then_inc(h_ready, 1)

            D0, EX, S0, D1, GE, PR = range(6)
            te = lambda ap: ap.rearrange("p (t e) -> p t e", e=E)
            tie_bc = tie[:, :].rearrange("p (a e) -> p a e", a=1).to_broadcast([P, T, E])
            dve.wait_ge(consts, 1)
            dve.wait_ge(logit_ps, 1)
            settle(V.tensor_reduce(rs[:, 0, :], te(pLogit), AX.X, ALU.max))
            V.tensor_tensor(te(rt[:, D0, :]), te(pLogit), over_e(rs[:, 0, :]), ALU.subtract).then_inc(d_ready, 1)
            dve.wait_ge(d_ready, 1)
            settle(V.scalar_tensor_tensor(te(rt[:, S0, :]), te(rt[:, D0, :]), 0.0, tie_bc, ALU.is_ge, ALU.mult))
            settle(V.tensor_reduce(rs[:, 1, :], te(rt[:, S0, :]), AX.X, ALU.max))
            settle(V.tensor_tensor(te(mk[:, 0, :]), te(rt[:, S0, :]), over_e(rs[:, 1, :]), ALU.is_equal))
            settle(V.scalar_tensor_tensor(rt[:, D1, :], mk[:, 0, :], -BIG, rt[:, D0, :], ALU.mult, ALU.add))
            settle(V.tensor_reduce(rs[:, 2, :], te(rt[:, D1, :]), AX.X, ALU.max))
            settle(V.tensor_tensor(te(rt[:, GE, :]), te(rt[:, D1, :]), over_e(rs[:, 2, :]), ALU.is_ge))
            settle(V.tensor_tensor(te(rt[:, GE, :]), te(rt[:, GE, :]), tie_bc, ALU.mult))
            settle(V.tensor_reduce(rs[:, 3, :], te(rt[:, GE, :]), AX.X, ALU.max))
            settle(V.tensor_tensor(te(mk[:, 1, :]), te(rt[:, GE, :]), over_e(rs[:, 3, :]), ALU.is_equal))
            gte = lambda ap: ap.rearrange("p (g t e) -> p g t e", g=GROUPS, e=E)
            get = lambda ap: ap.rearrange("p (g e t) -> p g t e", g=GROUPS, e=E)
            settle(V.tensor_tensor(get(both[:, :]), gte(mk[:, 0, :]), gte(mk[:, 1, :]), ALU.add))
            settle(V.tensor_tensor_scan(scan[:, 1:], ones[:, :], both[:, :], 0.0, ALU.mult, ALU.add))
            ends, starts = scan[:, TG:GROUPS * E * TG + 1:TG], scan[:, 0:GROUPS * E * TG:TG]
            V.tensor_tensor(cnt[:, 0, :], ends, starts, ALU.subtract).then_inc(runs_ready, 1)
            settle(V.tensor_tensor(cnt[:, 1, :], first[:, :], starts, ALU.subtract))
            dve.wait_ge(count_ps, 1)
            settle(V.tensor_tensor(cnt[:, 1, :], cnt[:, 1, :], pCount[:, 0:GROUPS * E], ALU.add))
            settle(V.tensor_tensor(both[:, :].rearrange("p (j t) -> p j t", t=TG), scan[:, 1:].rearrange("p (j t) -> p j t", t=TG),
                                   cnt[:, 1, :].rearrange("p (j a) -> p j a", a=1).to_broadcast([P, GROUPS * E, TG]), ALU.add))
            for k in range(TOPK):
                settle(V.tensor_tensor(gte(rt[:, S0, :]), get(both[:, :]), gte(mk[:, k, :]), ALU.mult))
                settle(V.tensor_reduce(rs[:, 6, :], te(rt[:, S0, :]), AX.X, ALU.add))
                V.tensor_copy(place[:, k, :], rs[:, 6, :]).then_inc(place_ready, 1)
                dve.wait_ge(place_ready, k + 1)
            dve.wait_ge(exp_ready, 1)
            settle(V.tensor_reduce(rs[:, 4, :], te(rt[:, EX, :]), AX.X, ALU.add))
            settle(V.reciprocal(rs[:, 5, :], rs[:, 4, :]))
            settle(V.tensor_tensor(te(rt[:, PR, :]), te(rt[:, EX, :]), over_e(rs[:, 5, :]), ALU.mult))
            for k in range(TOPK):
                settle(V.tensor_tensor(rt[:, S0, :], rt[:, PR, :], mk[:, k, :], ALU.mult))
                settle(V.tensor_reduce(gate[:, k, :], te(rt[:, S0, :]), AX.X, ALU.add))
            settle(V.tensor_tensor(rs[:, 6, :], gate[:, 0, :], gate[:, 1, :], ALU.add))
            settle(V.reciprocal(rs[:, 7, :], rs[:, 6, :]))
            V.tensor_tensor(gate[:, 1, :], gate[:, 1, :], rs[:, 7, :], ALU.mult)
            V.tensor_tensor(H[:, :, D], gate[:, 0, :], rs[:, 7, :], ALU.mult).then_inc(gate_ready, 1)

            total = pCount[0:1, GROUPS * E:2 * GROUPS * E]
            settle(V.scalar_tensor_tensor(tt[:, 5, :], first[0:1, :], 1.0, total, ALU.add, ALU.add))
            V.tensor_copy(fill_at[:, :], tt[:, 5, :]).then_inc(fill_ready, 1)
            settle(V.tensor_scalar(tt[:, 0, :], total, float(P - 1), None, ALU.add))
            settle(V.tensor_copy(tt_i[:, 0, :], tt[:, 0, :]))
            settle(V.tensor_scalar(tt_i[:, 1, :], tt_i[:, 0, :], P.bit_length() - 1, P.bit_length() - 1,
                                   ALU.logical_shift_right, ALU.logical_shift_left))
            settle(V.tensor_copy(tt[:, 2, :], tt_i[:, 1, :]))
            for g in range(GROUPS):
                j = slice(g * E, (g + 1) * E)
                settle(V.tensor_tensor_scan(tt[:, 3, j], ones[0:1, 0:E], tt[:, 2, j], 0.0, ALU.mult, ALU.add))
            settle(V.tensor_scalar(tt[:, 4, :], tt[:, 2, :], -1.0, float(REGION), ALU.mult, ALU.add))
            for g in range(GROUPS):
                z = slice(g * E + E - 1, g * E + E)
                settle(V.scalar_tensor_tensor(tt[:, 4, z], tt[:, 3, z], float(-P * MIN_TILES), tt[:, 4, z], ALU.add, ALU.add))
            for g in range(GROUPS):
                j = slice(g * E, (g + 1) * E)
                ie = lambda ap: ap.rearrange("p (i e) -> p i e", e=E)
                per_tile = at[:, :].rearrange("p (i a) -> p i a", a=1).to_broadcast([1, TILES, E])
                per_expert = lambda n: tt[:, n, j].rearrange("p (a e) -> p a e", a=1).to_broadcast([1, TILES, E])
                settle(V.tensor_tensor(ie(tw[:, 0, :]), per_tile, per_expert(3), ALU.is_ge))
                settle(V.tensor_tensor(ie(tw[:, 1, :]), ie(tw[:, 0, :]), per_expert(4), ALU.mult))
                settle(V.tensor_reduce(tn[:, 0, :], ie(tw[:, 0, :]), AX.X, ALU.add))
                settle(V.tensor_reduce(tn[:, 1, :], ie(tw[:, 1, :]), AX.X, ALU.add))
                tiles = slice(g * TILES, (g + 1) * TILES)
                V.tensor_scalar(tn[:, 2, :], tn[:, 0, :], float(E - 1), float(FF), ALU.min, ALU.mult)
                settle(V.scalar_tensor_tensor(tn[:, 3, :], tn[:, 1, :], float(g * GROUP_ROWS), at[:, :], ALU.add, ALU.add))
                V.tensor_copy(expert_of[:, tiles], tn[:, 2, :])
                last = V.tensor_copy(row_of[:, tiles], tn[:, 3, :])
                settle(last)
            V.tensor_copy(tn[:, 0, 0:1], tn[:, 1, 0:1]).then_inc(tiles_ready, 1)

            dve.wait_ge(w_hi, 2)
            V.tensor_tensor(W2l[:, :], raw2, W2h[:, :].bitcast(fp32), ALU.subtract).then_inc(w_lo, 1)
            V.memset(rawb, 0.0).then_inc(bias_zero, 1)
            dve.wait_ge(w_hi, 3)
            for r in (32, 96):
                V.tensor_tensor(BIAS[r:r + 1, :], rawb[r:r + 1, :], BIAS[r:r + 1, :].bitcast(fp32), ALU.subtract).then_inc(w_lo, 1)

            def step(turn, k):
                i = turn * RING + k
                if not isinstance(i, int) or i < NT:
                    dve.wait_ge(tile_hi, i + 1)
                    V.tensor_tensor(hTl[:, k % 2, :], pTile[k % 2], hTh[:, k % 2, :].bitcast(fp32), ALU.subtract).then_inc(tile_lo, 1)
                if later(i, 2) and (not isinstance(i, int) or i - 2 < NT):
                    dve.wait_ge(g_hi, i - 1)
                    V.tensor_tensor(gTl[:, k % 2, :], pGT[k % 2], gTh[:, k % 2, :].bitcast(fp32), ALU.subtract).then_inc(g_lo, 1)
                if later(i, 3):
                    m = k - 3
                    dve.wait_ge(y_ps, i - 2)
                    if later(i, 7):
                        dve.wait_ge(returned[m % 4], 16 * (2 * turn + (m + 8) // 4 - 2))
                    V.tensor_scalar(y[:, m % 4, :], pY[m % 2], tile_in[:, m % RING, D:D + 1], None, ALU.mult).then_inc(y_sb, 1)

            each_tile(dve, NT + 3, NT // RING, step)

            for c in range(NCH):
                t = slice(c * CHUNK, (c + 1) * CHUNK)
                dve.wait_ge(back_in[c][0], 16)
                dve.wait_ge(back_in[c][1], 16)
                settle(V.tensor_tensor(Z[:, t, :], Z[:, t, :], Q[:, t, :], ALU.add))
                V.tensor_tensor(X[:, t, :], X[:, t, :], Z[:, t, :], ALU.add).then_inc(out_ready, 1)

        @block.tensor
        def _(pe):
            mm = nc.tensor.matmul
            pe.wait_ge(consts, 1)
            pe.wait_ge(se_in, 16)
            nc.tensor.transpose(pSeT, se[:, :], ident[:, :]).then_inc(seT_ps, 1)
            pe.wait_ge(style_in, 16 * 8)
            pe.wait_ge(seT_sb, 1)
            mm(pHyp1, w_hyp1[:, :], seT[:, :], start=True, stop=True).then_inc(hyp1_ps, 1)
            pe.wait_ge(hyp1_sb, 1)
            mm(pHyp2, w_hyp2[:, :], hyp1T[:, :], start=True, stop=True).then_inc(hyp2_ps, 1)
            pe.wait_ge(hyp2_sb, 1)
            mm(pSty1, w_sty1[:, :], hyp2T[:, :], start=True, stop=True).then_inc(sty1_ps, 1)
            pe.wait_ge(sty1_sb, 1)
            mm(pSty, sty1T[:, :], w_sty2[:, :], start=True, stop=False)
            mm(pSty, ones[0:1, 0:P], b_sty2[:, :], start=False, stop=True).then_inc(sty_ps, 1)
            for n in range(T // 4):
                pe.wait_ge(z_ready, 4 * n // CHUNK + 1)
                last = mm(pMean, ident[:, :], Z[:, 4 * n:4 * n + 4, :].rearrange("p t d -> p (t d)"), start=(n == 0), stop=(n == T // 4 - 1))
            last.then_inc(mean_ps, 1)
            for n in range(T // 4):
                pe.wait_ge(sq_ready, n + 1)
                last = mm(pVar, ident[:, :], Q[:, 4 * n:4 * n + 4, :].rearrange("p t d -> p (t d)"), start=(n == 0), stop=(n == T // 4 - 1))
            last.then_inc(var_ps, 1)
            pe.wait_ge(norm_in, 16 * 3)
            for n in range(T // 4 + 1):
                if n < T // 4:
                    pe.wait_ge(h_ready, n + 1)
                    if n >= 4:
                        pe.wait_ge(hT_sb, n - 3)
                    for a in range(4):
                        last = nc.tensor.transpose(pHT[n % 4][:, a * P:(a + 1) * P], H[:, 4 * n + a, 0:D], ident[:, :])
                    last.then_inc(hT_ps, 1)
                if n >= 1:
                    pe.wait_ge(hT_sb, n)
                    for t in range(4 * n - 4, 4 * n):
                        last = mm(pLogit[:, t * E:(t + 1) * E], Q[:, t, :], w_router[:, :], start=True, stop=True)
            last.then_inc(logit_ps, 1)
            pe.wait_ge(runs_ready, 1)
            mm(pCount[:, 0:GROUPS * E], lower[:, :], cnt[:, 0, :], start=True, stop=True)
            mm(pCount[:, GROUPS * E:], ones[:, 0:P], cnt[:, 0, :], start=True, stop=True).then_inc(count_ps, 1)

            pe.wait_ge(tiles_ready, 1)
            pe.wait_ge(w_hi, 3)
            pe.wait_ge(w_lo, 4)

            def weights_of(i):
                return pe.value_load(expert_of[0:1, bass.ds(i, 1)], min_val=0, max_val=(E - 1) * FF)

            def turn_rows(turn, k):
                i = turn * RING + k
                pe.wait_ge(loaded[k], 16 * (turn + 1))
                if later(i, 2):
                    pe.wait_ge(tile_lo, i - 1)
                nc.tensor.transpose(pTile[k % 2], tile_in[:, k, 0:D], ident[:, :]).then_inc(tile_ps, 1)

            def first_product(i, k):
                w = weights_of(i)
                if later(i, 2):
                    pe.wait_ge(hid_sb, i - 1)
                mm(pHid[k % 2], pick1[:, :], BIAS[:, bass.ds(w, FF)], start=True, stop=False)
                pe.wait_ge(tile_hi, i + 1)
                mm(pHid[k % 2], hTh[:, k % 2, :], W1h[:, bass.ds(w, FF)], start=False, stop=False)
                mm(pHid[k % 2], hTh[:, k % 2, :], W1l[:, bass.ds(w, FF)], start=False, stop=False)
                pe.wait_ge(tile_lo, i + 1)
                mm(pHid[k % 2], hTl[:, k % 2, :], W1h[:, bass.ds(w, FF)], start=False, stop=True).then_inc(hid_ps, 1)

            def turn_hidden(i, k):
                pe.wait_ge(hid_sb, i + 1)
                if later(i, 2):
                    pe.wait_ge(g_lo, i - 1)
                for c in range(FC):
                    last = nc.tensor.transpose(pGT[k % 2][:, c * P:(c + 1) * P], hid[:, k % 2, c * P:(c + 1) * P], ident[:, :])
                last.then_inc(g_ps, 1)

            def second_product(i, k):
                w = weights_of(i)
                if later(i, 2):
                    pe.wait_ge(y_sb, i - 1)
                mm(pY[k % 2], pick2[:, :], BIAS[:, bass.ds(w, D)], start=True, stop=False)
                pe.wait_ge(g_hi, i + 1)
                for c in range(FC):
                    f = slice(c * P, (c + 1) * P)
                    mm(pY[k % 2], gTh[:, k % 2, f], W2h[:, bass.ds(w + c * D, D)], start=False, stop=False)
                    mm(pY[k % 2], gTh[:, k % 2, f], W2l[:, bass.ds(w + c * D, D)], start=False, stop=False)
                pe.wait_ge(g_lo, i + 1)
                for c in range(FC):
                    f = slice(c * P, (c + 1) * P)
                    last = mm(pY[k % 2], gTl[:, k % 2, f], W2h[:, bass.ds(w + c * D, D)], start=False, stop=(c == FC - 1))
                last.then_inc(y_ps, 1)

            def step(turn, k):
                i = turn * RING + k
                if not isinstance(i, int) or i < NT:
                    turn_rows(turn, k)
                if later(i, 1) and (not isinstance(i, int) or i - 1 < NT):
                    first_product(i - 1, k - 1)
                if later(i, 2) and (not isinstance(i, int) or i - 2 < NT):
                    turn_hidden(i - 2, k)
                if later(i, 3):
                    second_product(i - 3, k - 3)

            each_tile(pe, NT + 3, NT // RING, step)


_INS = ['x', 'itok_B_6_14', 'L0_cond_ln_g', 'L0_cond_ln_b', 'L0_cond_subj_emb', 'L0_cond_hyp_w1', 'L0_cond_hyp_b1',
        'L0_cond_hyp_w2', 'L0_cond_hyp_b2', 'L0_cond_sty_w1', 'L0_cond_sty_b1', 'L0_cond_sty_w2', 'L0_cond_sty_b2',
        'L0_cond_router_w', 'L0_cond_exp_w1', 'L0_cond_exp_b1', 'L0_cond_exp_w2', 'L0_cond_exp_b2']


def kernel(**inputs):
    import numpy as _np
    import concourse.bacc as _bacc
    from concourse import mybir as _mybir
    from concourse.bass_utils import run_bass_kernel_spmd as _run

    nc = _bacc.Bacc("TRN2", target_bir_lowering=False, num_devices=1)
    arrays, args = {}, []
    for name in _INS:
        a = _np.ascontiguousarray(inputs[name])
        arrays[f"in_{name}_dram"] = a
        args.append(nc.dram_tensor(f"in_{name}_dram", a.shape, _mybir.dt.from_np(a.dtype), kind="ExternalInput").ap())
    args.append(nc.dram_tensor("out_0_dram", (B, T, D), _mybir.dt.float32, kind="ExternalOutput").ap())
    conditional_moe_kernel(nc, *args)
    r = _run(nc, [arrays], core_ids=[0])
    return r.results[0]["out_0_dram"]
```

```python
import concourse.bass as bass
from concourse import mybir
from contextlib import ExitStack

B, T, D = 128, 32, 128
E, FF = 8, 512
SE, SH, S2 = 64, 128, 64
P = 128
FC = FF // P
TOPK = 2
GROUP_T = (12, 20)
GROUPS = len(GROUP_T)
T0 = (0, 12, 32)
LOAD_T = 8
CHUNK = 4
NCH = T // CHUNK
ROW = D + 2
MIN_TILES = [TOPK * n * B // P for n in GROUP_T]
TILES = [m + E - 1 for m in MIN_TILES]
NT = sum(TILES)
REGION = [n * B + P for n in GROUP_T]
GROUP_ROWS = [E * r + (E - 1) * P for r in REGION]
GROUP_AT = [0, GROUP_ROWS[0]]
TABLE_ROWS = sum(GROUP_ROWS)
AHEAD = 10
SPREAD = TILES[0] - 6
MEAN_PE, VAR_PE = 5, 5
NOWHERE = 1 << 20
RING = 8
EPS_LN, EPS_IN, EPS_SP = 1e-5, 1e-8, 1e-8
BIG = 1e30


def later(i, n):
    return i >= n if isinstance(i, int) else True


def is_tile(i):
    return 0 <= i < NT if isinstance(i, int) else True


def each_tile(eng, n_tiles, step):
    for k in range(RING):
        step(0, k)
    with eng.Fori(1, NT // RING, 1) as turn:
        for k in range(RING):
            step(turn, k)
    for i in range(NT // RING * RING, n_tiles):
        step(i // RING, i % RING)


def conditional_moe_kernel(nc, x, ids, ln_g, ln_b, subj_emb, hyp_w1, hyp_b1, hyp_w2, hyp_b2,
                           sty_w1, sty_b1, sty_w2, sty_b2, router_w, exp_w1, exp_b1, exp_w2, exp_b2, out):
    fp32, f32r, i32 = mybir.dt.float32, mybir.dt.float32r, mybir.dt.int32
    ALU, ACT, AX = mybir.AluOpType, mybir.ActivationFunctionType, mybir.AxisListType

    ctx = ExitStack()
    with ctx:
        def sb(name, shape, dt=fp32):
            return ctx.enter_context(nc.sbuf_tensor(name, shape, dt))

        def sem(name):
            return ctx.enter_context(nc.semaphore(name))

        rows = nc.dram_tensor("rows", [TABLE_ROWS, ROW], fp32, kind="Internal").ap()
        results = nc.dram_tensor("results", [TOPK * B * T, D], fp32, kind="Internal").ap()

        X = sb("X", [P, T, D])
        Z = sb("Z", [P, T, D])
        Q = sb("Q", [P, T, D])
        H = sb("H", [P, T, ROW])
        raw2 = Z[:, :, :].rearrange("p t d -> p (t d)")
        W1h, W1l = sb("W1h", [P, E * FF], f32r), sb("W1l", [P, E * FF], f32r)
        W2 = sb("W2", [P, E * FC, 2, D], f32r)
        B1 = sb("B1", [P, E * FF])
        raw1 = B1[:, :]
        B2 = sb("B2", [P, E * D], f32r)
        pick2 = sb("pick2", [P, P], f32r)
        pickf = sb("pickf", [P, P])
        ident = sb("ident", [P, P])
        lower = sb("lower", [P, P])
        ones = sb("ones", [P, max(GROUP_T) * E])
        filling = sb("filling", [P, ROW])
        idx = sb("idx", [P, 1], i32)
        se = sb("se", [P, SE])
        seT = sb("seT", [SE, P])
        hyp1T = sb("hyp1T", [SH, P])
        hyp2T = sb("hyp2T", [SH, P])
        sty1T = sb("sty1T", [S2, P])
        w_hyp1 = sb("w_hyp1", [SE, SH])
        w_hyp2 = sb("w_hyp2", [SH, SH])
        w_sty1 = sb("w_sty1", [SH, S2])
        w_sty2 = sb("w_sty2", [S2, 2 * D])
        b_hyp1 = sb("b_hyp1", [SH, 1])
        b_hyp2 = sb("b_hyp2", [SH, 1])
        b_sty1 = sb("b_sty1", [S2, 1])
        b_sty2 = sb("b_sty2", [1, 2 * D])
        w_router = sb("w_router", [D, E])
        gB = sb("gB", [P, D])
        bB = sb("bB", [P, D])
        stats = sb("stats", [P, T, 6])
        st = sb("st", [P, 6, T])
        gam = sb("gam", [P, 4, D])
        co = sb("co", [P, 10, D])
        mk = sb("mk", [P, TOPK, T * E])
        rt = sb("rt", [P, 6, T * E])
        rs = sb("rs", [P, 12, T])
        gate = sb("gate", [P, TOPK, T])
        tie = sb("tie", [P, E])
        tie_i = sb("tie_i", [P, E], i32)
        both = sb("both", [P, E * T])
        scan = sb("scan", [P, GROUPS + E * T])
        cnt = sb("cnt", [P, 4, GROUPS * E])
        first = sb("first", [P, GROUPS * E])
        first_i = sb("first_i", [P, GROUPS * E], i32)
        place = sb("place", [P, TOPK, T], i32)
        tt = sb("tt", [1, 6, GROUPS * E])
        tt_i = sb("tt_i", [1, 2, GROUPS * E], i32)
        tw = sb("tw", [1, 2, max(TILES) * E])
        at = sb("at", [1, max(TILES)])
        at_i = sb("at_i", [1, max(TILES)], i32)
        tn = sb("tn", [1, 4, max(TILES)])
        row_of = sb("row_of", [1, NT], i32)
        expert_of = sb("expert_of", [1, NT], i32)
        expert2_of = sb("expert2_of", [1, NT], i32)
        fill_at = sb("fill_at", [1, GROUPS * E], i32)
        tile_in = sb("tile_in", [P, RING, ROW])
        hTh, hTl = sb("hTh", [P, 2, P], f32r), sb("hTl", [P, 2, P], f32r)
        hid = sb("hid", [P, 2, FF])
        b2raw = hid[:, :, :].rearrange("p n f -> p (n f)")[:, 0:E * D]
        gTh, gTl = sb("gTh", [P, 2, FF], f32r), sb("gTl", [P, 2, FF], f32r)
        y = sb("y", [P, 4, D])

        ps = ctx.enter_context(nc.psum_tensor("ps", [P, 8, 512], fp32))
        pSeT, pHyp1, pHyp2, pSty1 = ps[0:SE, 0, 0:P], ps[0:SH, 0, P:2 * P], ps[0:SH, 0, 2 * P:3 * P], ps[0:S2, 0, 3 * P:4 * P]
        pSty = ps[:, 1, 0:2 * D]
        pMean, pVar = ps[:, 2, :], ps[:, 3, :]
        pLogit = ps[:, 1, 2 * D:2 * D + T * E]
        pCount = ps[:, 0, 0:2 * GROUPS * E]
        pHT = [ps[:, 4 + n, :] for n in range(4)]
        pHid, pGT = [ps[:, n, :] for n in range(2)], [ps[:, 2 + n, :] for n in range(2)]
        pTile, pY = [ps[:, 4 + n, 0:P] for n in range(2)], [ps[:, 6 + n, 0:2 * D] for n in range(2)]

        x_in = [sem(f"x_in{c}") for c in range(T // LOAD_T)]
        ids_in, se_in, style_in, norm_in = sem("ids_in"), sem("se_in"), sem("style_in"), sem("norm_in")
        w1_in, w2_in, b1_in, b2_in = sem("w1_in"), sem("w2_in"), sem("b1_in"), sem("b2_in")
        ident_ready, consts, b2_zero = sem("ident_ready"), sem("consts"), sem("b2_zero")
        pool_step, dve_step, act_step = sem("pool_step"), sem("dve_step"), sem("act_step")
        seT_ps, seT_sb, hyp1_ps, hyp1_sb, hyp2_ps, hyp2_sb, sty1_ps, sty1_sb, sty_ps = (
            sem(n) for n in ("seT_ps", "seT_sb", "hyp1_ps", "hyp1_sb", "hyp2_ps", "hyp2_sb", "sty1_ps", "sty1_sb", "sty_ps"))
        gamma_ln = sem("gamma_ln")
        var_ready, sd_ready, rsd_ready, z_ready, z_act, mean_ps = (
            sem(n) for n in ("var_ready", "sd_ready", "rsd_ready", "z_ready", "z_act", "mean_ps"))
        zc_ready, sq_ready, var_ps, vt_ready, sdt_ready = (
            sem(n) for n in ("zc_ready", "sq_ready", "var_ps", "vt_ready", "sdt_ready"))
        h_ready, hT_ps, hT_sb, logit_ps = sem("h_ready"), sem("hT_ps"), sem("hT_sb"), sem("logit_ps")
        d_ready, exp_ready, runs_ready, count_ps = sem("d_ready"), sem("exp_ready"), sem("runs_ready"), sem("count_ps")
        second_ready = sem("second_ready")
        place_ready, gate_ready, fill_ready, tiles_ready = (
            sem(n) for n in ("place_ready", "gate_ready", "fill_ready", "tiles_ready"))
        w1_hi, w1_lo, w2_hi, w2_lo, b2_hi, b2_lo = (
            sem(n) for n in ("w1_hi", "w1_lo", "w2_hi", "w2_lo", "b2_hi", "b2_lo"))
        sent = [[sem(f"sent{c}_{k}") for k in range(TOPK)] for c in range(NCH)]
        filled = [sem(f"filled{g}") for g in range(GROUPS)]
        loaded = [sem(f"loaded{n}") for n in range(RING)]
        returned = [sem(f"returned{n}") for n in range(4)]
        to_return = sem("to_return")
        tile_ps, tile_hi, tile_lo = sem("tile_ps"), sem("tile_hi"), sem("tile_lo")
        hid_ps, hid_sb, g_ps, g_hi, g_lo, y_ps, y_half, y_sb = (
            sem(n) for n in ("hid_ps", "hid_sb", "g_ps", "g_hi", "g_lo", "y_ps", "y_half", "y_sb"))
        back_in = [[sem(f"back{c}_{k}") for k in range(TOPK)] for c in range(NCH)]
        sum_ready, out_early, out_ready, out_done = (
            sem(n) for n in ("sum_ready", "out_early", "out_ready", "out_done"))

        block = ctx.enter_context(nc.Block())

        def times_returned(turn, k):
            return 16 * (2 * turn + k // 4 + 1)

        chunks_of = [range(T0[g] // CHUNK, T0[g + 1] // CHUNK) for g in range(GROUPS)]
        res = results.rearrange("(k b t) d -> k b t d", k=TOPK, b=B)

        @block.sync
        def _(sp):
            for c in range(T // LOAD_T):
                t = slice(c * LOAD_T, (c + 1) * LOAD_T)
                sp.dma_start(X[:, t, :], x[:, t, :]).then_inc(x_in[c], 16)
            sp.wait_ge(style_in, 16 * 8)
            sp.wait_ge(se_in, 16)
            sp.dma_start(raw1.rearrange("d (e f) -> d e f", e=E), exp_w1.rearrange("e d f -> d e f")).then_inc(w1_in, 16)
            sp.wait_ge(b2_zero, 1)
            for r in (64, 96):
                sp.dma_start(b2raw[r:r + 1, :], exp_b2.rearrange("(a e) d -> a (e d)", a=1)).then_inc(b2_in, 16)

            def fill(g):
                sp.wait_ge(fill_ready, g + 1)
                for n in range(E - 1):
                    r = GROUP_AT[g] + E * REGION[g] + n * P
                    sp.dma_start(rows[r:r + P, :], filling[:, :]).then_inc(filled[g], 16)
                for e in range(E):
                    j = g * E + e
                    r = sp.value_load(fill_at[0:1, j:j + 1], min_val=0, max_val=TABLE_ROWS - P)
                    sp.dma_start(rows[bass.ds(r, P), :], filling[:, :]).then_inc(filled[g], 16)

            sp.wait_ge(consts, 1)
            fill(0)
            sp.wait_ge(h_ready, NCH)
            sp.dma_start(raw2.rearrange("p (n d) -> p n d", d=D),
                         exp_w2.rearrange("e (c p) d -> p (e c) d", p=P)).then_inc(w2_in, 16)
            fill(1)

            def load(turn, k):
                i = turn * RING + k
                r = sp.value_load(row_of[0:1, bass.ds(i, 1)], min_val=0, max_val=TABLE_ROWS - P)
                if later(turn, 1):
                    sp.wait_ge(returned[k % 4], times_returned(turn - 1, k))
                sp.dma_start(tile_in[:, k, :], rows[bass.ds(r, P), :]).then_inc(loaded[k], 16)

            def loads(first, last):
                lo, hi = max(-(-first // RING), 1), last // RING
                for i in range(first, min(lo * RING, last)):
                    load(i // RING, i % RING)
                if hi > lo:
                    with sp.Fori(lo, hi, 1) as turn:
                        for k in range(RING):
                            load(turn, k)
                for i in range(max(hi, lo) * RING, last):
                    load(i // RING, i % RING)

            def group_written(g):
                for c in chunks_of[g]:
                    for k in range(TOPK):
                        sp.wait_ge(sent[c][k], 16 * CHUNK)
                sp.wait_ge(filled[g], 16 * (2 * E - 1))

            def results_back(g):
                for c in chunks_of[g]:
                    t = slice(c * CHUNK, (c + 1) * CHUNK)
                    sp.dma_start(Z[:, t, :], res[0][:, t, :]).then_inc(back_in[c][0], 16)
                    sp.dma_start(Q[:, t, :], res[1][:, t, :]).then_inc(back_in[c][1], 16)

            def put_out(c):
                t = slice(c * CHUNK, (c + 1) * CHUNK)
                sp.dma_start(out[:, t, :], X[:, t, :]).then_inc(out_done, 16)

            sp.wait_ge(tiles_ready, 1)
            group_written(0)
            loads(0, TILES[0])
            sp.wait_ge(tiles_ready, 2)
            group_written(1)
            early = NT // RING * RING - 2 * RING
            loads(TILES[0], early)
            for n in range(4):
                sp.wait_ge(returned[n], 16 * len(range(n, TILES[0], 4)))
            sp.wait_ge(w2_lo, 1)
            results_back(0)
            loads(early, NT)
            for n, c in enumerate(chunks_of[0]):
                sp.wait_ge(out_early, n + 1)
                put_out(c)

            for n in range(4):
                sp.wait_ge(returned[n], 16 * len(range(n, NT, 4)))
            results_back(1)
            for n, c in enumerate(chunks_of[1]):
                sp.wait_ge(out_ready, n + 1)
                put_out(c)
            sp.wait_ge(out_done, 16 * NCH)

        @block.gpsimd
        def _(pool):
            steps = [0]

            def settle(ins):
                steps[0] += 1
                ins.then_inc(pool_step, 1)
                pool.wait_ge(pool_step, steps[0])

            settle(pool.memset(ident[:, :], 0.0))
            pool.affine_select(out=ident[:, :], in_=ident[:, :], compare_op=ALU.not_equal, fill=1.0,
                               base=0, pattern=[[-1, P]], channel_multiplier=1).then_inc(ident_ready, 1)
            pool.memset(ones[:, :], 1.0).then_inc(ident_ready, 1)
            pool.wait_ge(ids_in, 16)
            pool.indirect_dma_start(out=se[:, :], out_offset=None, in_=subj_emb[:, :],
                                    in_offset=bass.IndirectOffsetOnAxis(ap=idx[:, 0:1], axis=0)).then_inc(se_in, 16)
            pool.memset(lower[:, :], 1.0)
            pool.memset(scan[:, :], 0.0)
            pool.memset(pickf[:, :], 0.0)
            pool.memset(b2raw, 0.0).then_inc(b2_zero, 1)
            settle(pool.memset(filling[:, :], 0.0))
            for r in (64, 96):
                settle(pool.memset(pickf[r:r + 1, :], 1.0))
            pool.iota(filling[:, D + 1:D + 2].bitcast(i32), [[0, 1]], base=NOWHERE, channel_multiplier=0)
            pool.affine_select(out=lower[:, :], in_=lower[:, :], compare_op=ALU.is_gt, fill=0.0,
                               base=0, pattern=[[1, P]], channel_multiplier=-1)
            pool.iota(at_i[:, :], [[P, max(TILES)]], base=0, channel_multiplier=0)
            for g in range(GROUPS):
                pool.iota(first_i[:, g * E:(g + 1) * E], [[REGION[g], E]], base=GROUP_AT[g] - 1, channel_multiplier=0)
            settle(pool.iota(tie_i[:, :], [[-1, E]], base=E, channel_multiplier=0))
            pool.tensor_copy(at[:, :], at_i[:, :])
            pool.tensor_copy(first[:, :], first_i[:, :])
            pool.tensor_copy(pick2[:, :], pickf[:, :])
            pool.tensor_copy(tie[:, :], tie_i[:, :]).then_inc(consts, 1)

            settle(pool.iota(H[:, :, D + 1:D + 2].bitcast(i32), [[1, T], [0, 1]], base=0, channel_multiplier=T))

            def send(t, k):
                pool.indirect_dma_start(out=rows[:, :], out_offset=bass.IndirectOffsetOnAxis(ap=place[:, k, t:t + 1], axis=0),
                                        in_=H[:, t, :], in_offset=None).then_inc(sent[t // CHUNK][k], 16)

            def turn_over(c):
                pool.wait_ge(sent[c][0], 16 * CHUNK)
                t = slice(c * CHUNK, (c + 1) * CHUNK)
                pool.iota(H[:, t, D + 1:D + 2].bitcast(i32), [[1, CHUNK], [0, 1]], base=B * T + c * CHUNK, channel_multiplier=T)
                settle(pool.tensor_copy(H[:, t, D:D + 1], gate[:, 1, t].rearrange("p (t a) -> p t a", a=1)))

            def sends(g, which):
                n = GROUP_T[g]
                for s in which:
                    k, t = s // n, T0[g] + s % n
                    if s == 0:
                        pool.wait_ge(h_ready, T0[g + 1] // CHUNK)
                        pool.wait_ge(place_ready, 2 * g + 2)
                        pool.wait_ge(gate_ready, g + 1)
                    if k == 1 and t % CHUNK == 0:
                        turn_over(t // CHUNK)
                    send(t, k)

            limit = pool.to_reg(TOPK * B * T - 1)

            def give_back(turn, k):
                i = turn * RING + k
                pool.wait_ge(y_sb, i + 1)
                if not isinstance(i, int):
                    pool.sem_inc(to_return, 1)
                pool.indirect_dma_start(out=results[:, :],
                                        out_offset=bass.IndirectOffsetOnAxis(ap=tile_in[:, k, D + 1:D + 2].bitcast(i32), axis=0),
                                        in_=y[:, k % 4, :], in_offset=None,
                                        bounds_check=limit, oob_is_err=False).then_inc(returned[k % 4], 16)

            sends(0, range(TOPK * GROUP_T[0]))
            sends(1, range(AHEAD))
            left = TOPK * GROUP_T[1] - AHEAD
            for i in range(TILES[0]):
                give_back(i // RING, i % RING)
                done, now = (left * min(a, SPREAD) // SPREAD for a in (i, i + 1))
                sends(1, range(AHEAD + done, AHEAD + now))
            for i in range(TILES[0], -(-TILES[0] // RING) * RING):
                give_back(i // RING, i % RING)
            last_turns = (NT // RING - 1) * RING
            with pool.Fori(-(-TILES[0] // RING), NT // RING - 1, 1) as turn:
                for k in range(RING):
                    give_back(turn, k)
            for i in range(last_turns, NT):
                give_back(i // RING, i % RING)
                n, which = divmod(i - last_turns - 4, 2)
                if 0 <= n < len(chunks_of[0]):
                    c = chunks_of[0][n]
                    t = slice(c * CHUNK, (c + 1) * CHUNK)
                    if which == 0:
                        pool.wait_ge(back_in[c][0], 16)
                        pool.wait_ge(back_in[c][1], 16)
                        settle(pool.tensor_tensor(Z[:, t, :], Z[:, t, :], Q[:, t, :], ALU.add))
                    else:
                        pool.tensor_tensor(X[:, t, :], X[:, t, :], Z[:, t, :], ALU.add).then_inc(out_early, 1)

        @block.scalar
        def _(act):
            act.dma_start(idx[:, :], ids.rearrange("(b a) -> b a", a=1)).then_inc(ids_in, 16)
            act.dma_start(w_hyp1[:, :], hyp_w1).then_inc(style_in, 16)
            act.dma_start(w_hyp2[:, :], hyp_w2).then_inc(style_in, 16)
            act.dma_start(w_sty1[:, :], sty_w1).then_inc(style_in, 16)
            act.dma_start(w_sty2[:, :], sty_w2).then_inc(style_in, 16)
            act.dma_start(b_hyp1[:, :], hyp_b1.rearrange("(b a) -> b a", a=1)).then_inc(style_in, 16)
            act.dma_start(b_hyp2[:, :], hyp_b2.rearrange("(b a) -> b a", a=1)).then_inc(style_in, 16)
            act.dma_start(b_sty1[:, :], sty_b1.rearrange("(b a) -> b a", a=1)).then_inc(style_in, 16)
            act.dma_start(b_sty2[:, :], sty_b2.rearrange("(a b) -> a b", a=1)).then_inc(style_in, 16)
            act.dma_start(w_router[:, :], router_w).then_inc(norm_in, 16)
            act.dma_start(gB[:, :], ln_g.rearrange("(a b) -> a b", a=1).to_broadcast([P, D])).then_inc(norm_in, 16)
            act.dma_start(bB[:, :], ln_b.rearrange("(a b) -> a b", a=1).to_broadcast([P, D])).then_inc(norm_in, 16)

            def layer_sd(c):
                t = slice(c * LOAD_T, (c + 1) * LOAD_T)
                act.wait_ge(var_ready, c + 1)
                act.activation(st[:, 2, t], st[:, 1, t], ACT.Sqrt).then_inc(sd_ready, 1)

            def layer_norm(c):
                act.wait_ge(rsd_ready, c + 1)
                for t in range(c * LOAD_T + LOAD_T // 2, (c + 1) * LOAD_T):
                    last = act.activation(Z[:, t, :], X[:, t, :], ACT.Identity, scale=st[:, 3, t:t + 1], bias=st[:, 5, t:t + 1])
                last.then_inc(z_act, 1)

            layer_sd(0)
            act.wait_ge(style_in, 16 * 8)
            act.wait_ge(hyp1_ps, 1)
            act.activation(hyp1T[:, :], pHyp1, ACT.Relu, bias=b_hyp1[:, :]).then_inc(hyp1_sb, 1)
            layer_sd(1)
            layer_norm(0)
            act.wait_ge(hyp2_ps, 1)
            act.activation(hyp2T[:, :], pHyp2, ACT.Identity, bias=b_hyp2[:, :]).then_inc(hyp2_sb, 1)
            layer_sd(2)
            layer_norm(1)
            act.wait_ge(sty1_ps, 1)
            act.activation(sty1T[:, :], pSty1, ACT.Relu, bias=b_sty1[:, :]).then_inc(sty1_sb, 1)
            layer_sd(3)
            layer_norm(2)
            layer_norm(3)
            act.wait_ge(sty_ps, 1)
            act.activation(gam[:, 0, :], pSty[:, 0:D], ACT.Abs).then_inc(act_step, 1)
            act.wait_ge(act_step, 1)
            act.activation(gam[:, 1, :], gam[:, 0, :], ACT.Exp, scale=-1.0).then_inc(act_step, 1)
            act.wait_ge(act_step, 2)
            act.activation(gam[:, 2, :], gam[:, 1, :], ACT.Ln, bias=1.0).then_inc(gamma_ln, 1)
            for n in range(NCH):
                act.wait_ge(zc_ready, n + 1)
                act.activation(Q[:, 4 * n:4 * n + 4, :], Q[:, 4 * n:4 * n + 4, :], ACT.Square).then_inc(sq_ready, 1)
            act.wait_ge(vt_ready, 1)
            act.activation(co[:, 3, :], co[:, 2, :], ACT.Sqrt).then_inc(sdt_ready, 1)

            def turned_out(g):
                for n in chunks_of[g]:
                    act.wait_ge(hT_ps, n + 1)
                    act.activation(Q[:, 4 * n:4 * n + 4, :], pHT[n % 4].rearrange("p (t d) -> p t d", d=P), ACT.Copy).then_inc(hT_sb, 1)

            def exponentials(g):
                te = slice(T0[g] * E, T0[g + 1] * E)
                t = slice(T0[g], T0[g + 1])
                act.wait_ge(d_ready, g + 1)
                act.activation(rt[:, 1, te], rt[:, 0, te], ACT.Exp)
                act.wait_ge(second_ready, g + 1)
                act.activation(rs[:, 8, t], rs[:, 2, t], ACT.Exp).then_inc(exp_ready, 1)

            act.wait_ge(var_ps, 1)
            act.wait_ge(vt_ready, 1)
            turned_out(0)
            exponentials(0)
            act.wait_ge(b2_in, 16 * 2)
            act.activation(B2[:, :], b2raw, ACT.Copy).then_inc(b2_hi, 1)
            act.wait_ge(w1_in, 16)
            act.activation(W1h[:, :], raw1, ACT.Copy).then_inc(w1_hi, 1)
            turned_out(1)
            exponentials(1)
            act.wait_ge(w1_lo, 1)
            act.dma_start(B1[:, :], exp_b1.rearrange("(a e) f -> a (e f)", a=1).to_broadcast([P, E * FF])).then_inc(b1_in, 16)
            act.wait_ge(w2_in, 16)
            act.activation(W2[:, :, 0, :], raw2.rearrange("p (n d) -> p n d", d=D), ACT.Copy).then_inc(w2_hi, 1)

            def step(turn, k):
                i = turn * RING + k
                if is_tile(i):
                    act.wait_ge(tile_ps, i + 1)
                    if later(i, 2):
                        act.wait_ge(hid_ps, i - 1)
                    act.activation(hTh[:, k % 2, :], pTile[k % 2], ACT.Copy).then_inc(tile_hi, 1)
                if is_tile(i - 2):
                    act.wait_ge(g_ps, i - 1)
                    if later(i, 4):
                        act.wait_ge(y_ps, i - 3)
                    act.activation(gTh[:, k % 2, :], pGT[k % 2], ACT.Relu).then_inc(g_hi, 1)
                if is_tile(i - 3):
                    m = k - 3
                    act.wait_ge(y_ps, i - 2)
                    if later(i, 7):
                        act.wait_ge(returned[m % 4], 16 * (2 * turn + (m + 8) // 4 - 2))
                    act.activation(y[:, m % 4, :], pY[m % 2][:, 0:D], ACT.Copy, scale=tile_in[:, m % RING, D:D + 1]).then_inc(y_half, 1)

            each_tile(act, NT + 3, step)

        @block.vector
        def _(dve):
            steps = [0]

            def settle(ins):
                steps[0] += 1
                ins.then_inc(dve_step, 1)
                dve.wait_ge(dve_step, steps[0])

            def over_t(ap, n):
                return ap.rearrange("p (a d) -> p a d", a=1).to_broadcast([P, n, D])

            def over_e(ap, n):
                return ap.rearrange("p (t a) -> p t a", a=1).to_broadcast([P, n, E])

            V = nc.vector
            MEAN, VAR, SD, RSD, TMP, MRSD = range(6)

            def layer_stats(c):
                dve.wait_ge(x_in[c], 16)
                for t in range(c * LOAD_T, (c + 1) * LOAD_T):
                    last = V.bn_stats(stats[:, t, :], X[:, t, :])
                settle(last)
                t = slice(c * LOAD_T, (c + 1) * LOAD_T)
                me, mo, ve, vo = (stats[:, t, n] for n in (1, 4, 2, 5))
                V.tensor_tensor(st[:, MEAN, t], me, mo, ALU.add)
                V.tensor_tensor(st[:, VAR, t], ve, vo, ALU.add)
                settle(V.tensor_tensor(st[:, TMP, t], me, mo, ALU.subtract))
                V.tensor_scalar(st[:, MEAN, t], st[:, MEAN, t], 0.5, None, ALU.mult)
                V.tensor_scalar(st[:, VAR, t], st[:, VAR, t], 1.0 / D, EPS_LN, ALU.mult, ALU.add)
                settle(V.scalar_tensor_tensor(st[:, TMP, t], st[:, TMP, t], 0.25, st[:, TMP, t], ALU.mult, ALU.mult))
                V.tensor_tensor(st[:, VAR, t], st[:, VAR, t], st[:, TMP, t], ALU.add).then_inc(var_ready, 1)

            def layer_norm(c):
                t = slice(c * LOAD_T, (c + 1) * LOAD_T)
                dve.wait_ge(sd_ready, c + 1)
                settle(V.reciprocal(st[:, RSD, t], st[:, SD, t]))
                V.scalar_tensor_tensor(st[:, MRSD, t], st[:, MEAN, t], -1.0, st[:, RSD, t], ALU.mult, ALU.mult).then_inc(rsd_ready, 1)
                for t in range(c * LOAD_T, c * LOAD_T + LOAD_T // 2):
                    last = V.tensor_scalar(Z[:, t, :], X[:, t, :], st[:, MEAN, t:t + 1], st[:, RSD, t:t + 1], ALU.subtract, ALU.mult)
                last.then_inc(z_ready, 1)

            for c in range(T // LOAD_T + 1):
                if c < T // LOAD_T:
                    layer_stats(c)
                if c == 0:
                    dve.wait_ge(seT_ps, 1)
                    V.tensor_copy(seT[:, :], pSeT).then_inc(seT_sb, 1)
                if c >= 1:
                    layer_norm(c - 1)

            MZ, VZ, VT, SDT, RT, GG, MT, G2, A, C = range(10)
            dve.wait_ge(norm_in, 16 * 3)
            V.tensor_tensor(co[:, G2, :], gB[:, :], gB[:, :], ALU.mult)
            dve.wait_ge(z_act, T // LOAD_T)
            dve.wait_ge(z_ready, T // LOAD_T)
            V.tensor_reduce(co[:, RT, :], Z[:, 4 * MEAN_PE:, :].rearrange("p t d -> p d t"), AX.X, ALU.add)
            dve.wait_ge(mean_ps, 1)
            settle(V.tensor_reduce(co[:, MZ, :], pMean.rearrange("p (t d) -> p d t", d=D), AX.X, ALU.add))
            settle(V.tensor_tensor(co[:, MZ, :], co[:, MZ, :], co[:, RT, :], ALU.add))
            settle(V.tensor_scalar(co[:, MZ, :], co[:, MZ, :], 1.0 / T, None, ALU.mult))
            for n in range(NCH):
                V.tensor_tensor(Q[:, 4 * n:4 * n + 4, :], Z[:, 4 * n:4 * n + 4, :], over_t(co[:, MZ, :], 4), ALU.subtract).then_inc(zc_ready, 1)
            dve.wait_ge(gamma_ln, 1)
            settle(V.scalar_tensor_tensor(gam[:, 3, :], pSty[:, 0:D], 0.0, gam[:, 2, :], ALU.max, ALU.add))
            settle(V.tensor_scalar(gam[:, 3, :], gam[:, 3, :], EPS_SP, None, ALU.add))
            V.tensor_tensor(co[:, GG, :], gB[:, :], gam[:, 3, :], ALU.mult)
            settle(V.tensor_tensor(co[:, MT, :], co[:, MZ, :], gB[:, :], ALU.mult))
            settle(V.tensor_tensor(co[:, MT, :], co[:, MT, :], bB[:, :], ALU.add))
            settle(V.tensor_tensor(co[:, MT, :], bB[:, :], co[:, MT, :], ALU.subtract))
            V.tensor_tensor(co[:, MT, :], co[:, MT, :], gam[:, 3, :], ALU.mult)
            dve.wait_ge(sq_ready, NCH)
            V.tensor_reduce(co[:, RT, :], Q[:, 4 * VAR_PE:, :].rearrange("p t d -> p d t"), AX.X, ALU.add)
            dve.wait_ge(var_ps, 1)
            settle(V.tensor_reduce(co[:, VZ, :], pVar.rearrange("p (t d) -> p d t", d=D), AX.X, ALU.add))
            settle(V.tensor_tensor(co[:, VZ, :], co[:, VZ, :], co[:, RT, :], ALU.add))
            settle(V.scalar_tensor_tensor(co[:, VT, :], co[:, VZ, :], 1.0 / T, co[:, G2, :], ALU.mult, ALU.mult))
            V.tensor_scalar(co[:, VT, :], co[:, VT, :], EPS_IN, None, ALU.add).then_inc(vt_ready, 1)
            dve.wait_ge(sdt_ready, 1)
            settle(V.reciprocal(co[:, RT, :], co[:, SDT, :]))
            V.tensor_tensor(co[:, A, :], co[:, GG, :], co[:, RT, :], ALU.mult)
            settle(V.tensor_tensor(co[:, C, :], co[:, MT, :], co[:, RT, :], ALU.mult))
            settle(V.tensor_tensor(co[:, C, :], co[:, C, :], pSty[:, D:2 * D], ALU.add))

            def make_h(n):
                t = slice(4 * n, 4 * n + 4)
                settle(V.tensor_tensor(H[:, t, 0:D], Z[:, t, :], over_t(co[:, A, :], 4), ALU.mult))
                V.tensor_tensor(H[:, t, 0:D], H[:, t, 0:D], over_t(co[:, C, :], 4), ALU.add).then_inc(h_ready, 1)

            D0, EX, S0, D1, GE, S1 = range(6)

            def route(g):
                n, ts = GROUP_T[g], slice(T0[g], T0[g + 1])
                cols = slice(T0[g] * E, T0[g + 1] * E)
                te = lambda ap: ap[:, cols].rearrange("p (t e) -> p t e", e=E)
                e_t = lambda ap: ap.rearrange("p (e t) -> p t e", e=E)
                tie_bc = tie[:, :].rearrange("p (a e) -> p a e", a=1).to_broadcast([P, n, E])
                J = slice(g * E, (g + 1) * E)
                dve.wait_ge(logit_ps, g + 1)
                settle(V.tensor_reduce(rs[:, 0, ts], te(pLogit), AX.X, ALU.max))
                V.tensor_tensor(te(rt[:, D0, :]), te(pLogit), over_e(rs[:, 0, ts], n), ALU.subtract).then_inc(d_ready, 1)
                dve.wait_ge(d_ready, g + 1)
                settle(V.scalar_tensor_tensor(te(rt[:, S0, :]), te(rt[:, D0, :]), 0.0, tie_bc, ALU.is_ge, ALU.mult))
                settle(V.tensor_reduce(rs[:, 1, ts], te(rt[:, S0, :]), AX.X, ALU.max))
                settle(V.tensor_tensor(te(mk[:, 0, :]), te(rt[:, S0, :]), over_e(rs[:, 1, ts], n), ALU.is_equal))
                settle(V.scalar_tensor_tensor(rt[:, D1, cols], mk[:, 0, cols], -BIG, rt[:, D0, cols], ALU.mult, ALU.add))
                V.tensor_reduce(rs[:, 2, ts], te(rt[:, D1, :]), AX.X, ALU.max).then_inc(second_ready, 1)
                dve.wait_ge(second_ready, g + 1)
                settle(V.tensor_tensor(te(rt[:, GE, :]), te(rt[:, D1, :]), over_e(rs[:, 2, ts], n), ALU.is_ge))
                settle(V.tensor_tensor(te(rt[:, GE, :]), te(rt[:, GE, :]), tie_bc, ALU.mult))
                settle(V.tensor_reduce(rs[:, 3, ts], te(rt[:, GE, :]), AX.X, ALU.max))
                settle(V.tensor_tensor(te(mk[:, 1, :]), te(rt[:, GE, :]), over_e(rs[:, 3, ts], n), ALU.is_equal))
                both_g = both[:, cols]
                s0 = g + T0[g] * E
                scan_g = scan[:, s0 + 1:s0 + 1 + n * E]
                settle(V.tensor_tensor(e_t(both_g), te(mk[:, 0, :]), te(mk[:, 1, :]), ALU.add))
                settle(V.tensor_tensor_scan(scan_g, ones[:, 0:n * E], both_g, 0.0, ALU.mult, ALU.add))
                ends, starts = scan[:, s0 + n:s0 + n * E + 1:n], scan[:, s0:s0 + n * (E - 1) + 1:n]
                V.tensor_tensor(cnt[:, 0, J], ends, starts, ALU.subtract).then_inc(runs_ready, 1)
                V.tensor_tensor(cnt[:, 1, J], first[:, J], starts, ALU.subtract)
                dve.wait_ge(exp_ready, g + 1)
                settle(V.tensor_reduce(rs[:, 4, ts], te(rt[:, EX, :]), AX.X, ALU.add))
                settle(V.reciprocal(rs[:, 5, ts], rs[:, 4, ts]))
                settle(V.tensor_tensor(rs[:, 6, ts], rs[:, 8, ts], rs[:, 5, ts], ALU.mult))
                settle(V.tensor_tensor(rs[:, 7, ts], rs[:, 5, ts], rs[:, 6, ts], ALU.add))
                dve.wait_ge(count_ps, g + 1)
                V.tensor_tensor(cnt[:, 2, J], cnt[:, 1, J], pCount[:, J], ALU.add)
                settle(V.reciprocal(rs[:, 9, ts], rs[:, 7, ts]))
                V.tensor_tensor(gate[:, 1, ts], rs[:, 6, ts], rs[:, 9, ts], ALU.mult)
                V.tensor_tensor(H[:, ts, D], rs[:, 5, ts], rs[:, 9, ts], ALU.mult).then_inc(gate_ready, 1)
                settle(V.tensor_tensor(both_g.rearrange("p (j t) -> p j t", t=n), scan_g.rearrange("p (j t) -> p j t", t=n),
                                       cnt[:, 2, J].rearrange("p (j a) -> p j a", a=1).to_broadcast([P, E, n]), ALU.add))
                V.tensor_tensor(te(rt[:, S0, :]), e_t(both_g), te(mk[:, 0, :]), ALU.mult)
                settle(V.tensor_tensor(te(rt[:, S1, :]), e_t(both_g), te(mk[:, 1, :]), ALU.mult))
                V.tensor_reduce(rs[:, 10, ts], te(rt[:, S0, :]), AX.X, ALU.add)
                settle(V.tensor_reduce(rs[:, 11, ts], te(rt[:, S1, :]), AX.X, ALU.add))
                V.tensor_copy(place[:, 0, ts], rs[:, 10, ts]).then_inc(place_ready, 1)
                V.tensor_copy(place[:, 1, ts], rs[:, 11, ts]).then_inc(place_ready, 1)

            def list_tiles(g):
                J = slice(g * E, (g + 1) * E)
                total = pCount[0:1, GROUPS * E + g * E:GROUPS * E + (g + 1) * E]
                settle(V.scalar_tensor_tensor(tt[:, 5, J], first[0:1, J], 1.0, total, ALU.add, ALU.add))
                V.tensor_copy(fill_at[:, J], tt[:, 5, J]).then_inc(fill_ready, 1)
                settle(V.tensor_scalar(tt[:, 0, J], total, float(P - 1), None, ALU.add))
                settle(V.tensor_copy(tt_i[:, 0, J], tt[:, 0, J]))
                settle(V.tensor_scalar(tt_i[:, 1, J], tt_i[:, 0, J], P.bit_length() - 1, P.bit_length() - 1,
                                       ALU.logical_shift_right, ALU.logical_shift_left))
                settle(V.tensor_copy(tt[:, 2, J], tt_i[:, 1, J]))
                V.tensor_scalar(tt[:, 4, J], tt[:, 2, J], -1.0, float(REGION[g]), ALU.mult, ALU.add)
                settle(V.tensor_tensor_scan(tt[:, 3, J], ones[0:1, 0:E], tt[:, 2, J], 0.0, ALU.mult, ALU.add))
                z = slice(g * E + E - 1, g * E + E)
                settle(V.scalar_tensor_tensor(tt[:, 4, z], tt[:, 3, z], float(-P * MIN_TILES[g]), tt[:, 4, z], ALU.add, ALU.add))
                m = TILES[g]
                ie = lambda ap: ap[:, 0:m * E].rearrange("p (i e) -> p i e", e=E)
                per_tile = at[:, 0:m].rearrange("p (i a) -> p i a", a=1).to_broadcast([1, m, E])
                per_expert = lambda a: tt[:, a, J].rearrange("p (a e) -> p a e", a=1).to_broadcast([1, m, E])
                settle(V.tensor_tensor(ie(tw[:, 0, :]), per_tile, per_expert(3), ALU.is_ge))
                settle(V.tensor_tensor(ie(tw[:, 1, :]), ie(tw[:, 0, :]), per_expert(4), ALU.mult))
                V.tensor_reduce(tn[:, 0, 0:m], ie(tw[:, 0, :]), AX.X, ALU.add)
                settle(V.tensor_reduce(tn[:, 1, 0:m], ie(tw[:, 1, :]), AX.X, ALU.add))
                tiles = slice(sum(TILES[:g]), sum(TILES[:g + 1]))
                V.tensor_scalar(tn[:, 2, 0:m], tn[:, 0, 0:m], float(E - 1), float(FF), ALU.min, ALU.mult)
                settle(V.scalar_tensor_tensor(tn[:, 3, 0:m], tn[:, 1, 0:m], float(GROUP_AT[g]), at[:, 0:m], ALU.add, ALU.add))
                V.tensor_copy(expert_of[:, tiles], tn[:, 2, 0:m])
                V.tensor_scalar(expert2_of[:, tiles], tn[:, 2, 0:m], 2.0, None, ALU.mult)
                V.tensor_copy(row_of[:, tiles], tn[:, 3, 0:m]).then_inc(tiles_ready, 1)
                dve.wait_ge(tiles_ready, g + 1)

            dve.wait_ge(consts, 1)
            ahead = T0[1] // CHUNK + 2
            for n in range(ahead):
                make_h(n)
            route(0)
            for n in range(ahead, NCH):
                make_h(n)
            list_tiles(0)
            dve.wait_ge(w1_hi, 1)
            V.tensor_tensor(W1l[:, :], raw1, W1h[:, :].bitcast(fp32), ALU.subtract).then_inc(w1_lo, 1)
            route(1)
            list_tiles(1)
            dve.wait_ge(b2_hi, 1)
            V.tensor_tensor(B2[96:97, :], b2raw[96:97, :], B2[96:97, :].bitcast(fp32), ALU.subtract).then_inc(b2_lo, 1)
            dve.wait_ge(w2_hi, 1)
            V.tensor_tensor(W2[:, :, 1, :], raw2.rearrange("p (n d) -> p n d", d=D), W2[:, :, 0, :].bitcast(fp32), ALU.subtract).then_inc(w2_lo, 1)
            dve.wait_ge(b1_in, 16)

            def step(turn, k):
                i = turn * RING + k
                if is_tile(i):
                    dve.wait_ge(tile_hi, i + 1)
                    V.tensor_tensor(hTl[:, k % 2, :], pTile[k % 2], hTh[:, k % 2, :].bitcast(fp32), ALU.subtract).then_inc(tile_lo, 1)
                if is_tile(i - 1):
                    w = dve.value_load(expert_of[0:1, bass.ds(i - 1, 1)], min_val=0, max_val=(E - 1) * FF)
                    dve.wait_ge(hid_ps, i)
                    if later(i, 3):
                        dve.wait_ge(g_ps, i - 2)
                    V.tensor_tensor(hid[:, (k - 1) % 2, :], pHid[(k - 1) % 2], B1[:, bass.ds(w, FF)], ALU.add).then_inc(hid_sb, 1)
                if is_tile(i - 2):
                    dve.wait_ge(g_hi, i - 1)
                    V.scalar_tensor_tensor(gTl[:, k % 2, :], pGT[k % 2], 0.0, gTh[:, k % 2, :].bitcast(fp32), ALU.max, ALU.subtract).then_inc(g_lo, 1)
                if is_tile(i - 3):
                    m = k - 3
                    dve.wait_ge(y_half, i - 2)
                    V.scalar_tensor_tensor(y[:, m % 4, :], pY[m % 2][:, D:2 * D], tile_in[:, m % RING, D:D + 1], y[:, m % 4, :],
                                           ALU.mult, ALU.add).then_inc(y_sb, 1)

            each_tile(dve, NT + 3, step)

            for c in chunks_of[1]:
                t = slice(c * CHUNK, (c + 1) * CHUNK)
                dve.wait_ge(back_in[c][0], 16)
                dve.wait_ge(back_in[c][1], 16)
                settle(V.tensor_tensor(Z[:, t, :], Z[:, t, :], Q[:, t, :], ALU.add))
                V.tensor_tensor(X[:, t, :], X[:, t, :], Z[:, t, :], ALU.add).then_inc(out_ready, 1)

        @block.tensor
        def _(pe):
            mm = nc.tensor.matmul
            pe.wait_ge(ident_ready, 2)
            pe.wait_ge(se_in, 16)
            nc.tensor.transpose(pSeT, se[:, :], ident[:, :]).then_inc(seT_ps, 1)
            pe.wait_ge(style_in, 16 * 8)
            pe.wait_ge(seT_sb, 1)
            mm(pHyp1, w_hyp1[:, :], seT[:, :], start=True, stop=True).then_inc(hyp1_ps, 1)
            def sum_z(n):
                pe.wait_ge(z_act if n % 2 else z_ready, n // 2 + 1)
                return mm(pMean, ident[:, :], Z[:, 4 * n:4 * n + 4, :].rearrange("p t d -> p (t d)"), start=(n == 0), stop=(n == MEAN_PE - 1))

            pe.wait_ge(hyp1_sb, 1)
            mm(pHyp2, w_hyp2[:, :], hyp1T[:, :], start=True, stop=True).then_inc(hyp2_ps, 1)
            sum_z(0)
            pe.wait_ge(hyp2_sb, 1)
            mm(pSty1, w_sty1[:, :], hyp2T[:, :], start=True, stop=True).then_inc(sty1_ps, 1)
            for n in range(1, MEAN_PE):
                last = sum_z(n)
            last.then_inc(mean_ps, 1)
            pe.wait_ge(sty1_sb, 1)
            mm(pSty, sty1T[:, :], w_sty2[:, :], start=True, stop=False)
            mm(pSty, ones[0:1, 0:P], b_sty2[:, :], start=False, stop=True).then_inc(sty_ps, 1)
            for n in range(VAR_PE):
                pe.wait_ge(sq_ready, n + 1)
                last = mm(pVar, ident[:, :], Q[:, 4 * n:4 * n + 4, :].rearrange("p t d -> p (t d)"), start=(n == 0), stop=(n == VAR_PE - 1))
            last.then_inc(var_ps, 1)

            def turn_h(n):
                pe.wait_ge(h_ready, n + 1)
                if n >= 4:
                    pe.wait_ge(hT_sb, n - 3)
                for a in range(4):
                    last = nc.tensor.transpose(pHT[n % 4][:, a * P:(a + 1) * P], H[:, 4 * n + a, 0:D], ident[:, :])
                last.then_inc(hT_ps, 1)

            def logits(n):
                pe.wait_ge(hT_sb, n + 1)
                for t in range(4 * n, 4 * n + 4):
                    last = mm(pLogit[:, t * E:(t + 1) * E], Q[:, t, :], w_router[:, :], start=True, stop=True)
                return last

            pe.wait_ge(consts, 1)

            def counts(g):
                pe.wait_ge(runs_ready, g + 1)
                mm(pCount[:, g * E:(g + 1) * E], lower[:, :], cnt[:, 0, g * E:(g + 1) * E], start=True, stop=True)
                mm(pCount[:, (GROUPS + g) * E:(GROUPS + g + 1) * E], ones[:, 0:P], cnt[:, 0, g * E:(g + 1) * E],
                   start=True, stop=True).then_inc(count_ps, 1)

            pe.wait_ge(norm_in, 16 * 3)
            for g in range(GROUPS):
                for n in chunks_of[g]:
                    turn_h(n)
                    if n > chunks_of[g][0]:
                        logits(n - 1)
                logits(chunks_of[g][-1]).then_inc(logit_ps, 1)
                counts(g)

            pe.wait_ge(tiles_ready, 2)
            pe.wait_ge(w1_hi, 1)
            pe.wait_ge(w1_lo, 1)
            pe.wait_ge(b2_lo, 1)

            def weights_of(i):
                return pe.value_load(expert2_of[0:1, bass.ds(i, 1)], min_val=0, max_val=(E - 1) * 2 * FF)

            def turn_rows(turn, k):
                i = turn * RING + k
                pe.wait_ge(loaded[k], 16 * (turn + 1))
                if later(i, 2):
                    pe.wait_ge(tile_lo, i - 1)
                nc.tensor.transpose(pTile[k % 2], tile_in[:, k, 0:D], ident[:, :]).then_inc(tile_ps, 1)

            def first_product(i, k, w2):
                w = w2 // 2
                pe.wait_ge(tile_hi, i + 1)
                if later(i, 2):
                    pe.wait_ge(hid_sb, i - 1)
                mm(pHid[k % 2], hTh[:, k % 2, :], W1h[:, bass.ds(w, FF)], start=True, stop=False)
                mm(pHid[k % 2], hTh[:, k % 2, :], W1l[:, bass.ds(w, FF)], start=False, stop=False)
                pe.wait_ge(tile_lo, i + 1)
                mm(pHid[k % 2], hTl[:, k % 2, :], W1h[:, bass.ds(w, FF)], start=False, stop=True).then_inc(hid_ps, 1)

            def turn_hidden(i, k):
                pe.wait_ge(hid_sb, i + 1)
                if later(i, 2):
                    pe.wait_ge(g_lo, i - 1)
                for c in range(FC):
                    last = nc.tensor.transpose(pGT[k % 2][:, c * P:(c + 1) * P], hid[:, k % 2, c * P:(c + 1) * P], ident[:, :])
                last.then_inc(g_ps, 1)

            W2_flat = W2[:, :, :, :].rearrange("p n h d -> p (n h d)")

            def second_product(i, k, w2):
                pe.wait_ge(g_hi, i + 1)
                if later(i, 2):
                    pe.wait_ge(y_sb, i - 1)
                for c in range(FC):
                    mm(pY[k % 2], gTh[:, k % 2, c * P:(c + 1) * P], W2_flat[:, bass.ds(w2 + c * 2 * D, 2 * D)], start=(c == 0), stop=False)
                mm(pY[k % 2][:, 0:D], pick2[:, :], B2[:, bass.ds(w2 // 8, D)], start=False, stop=False)
                pe.wait_ge(g_lo, i + 1)
                for c in range(FC):
                    last = mm(pY[k % 2][:, 0:D], gTl[:, k % 2, c * P:(c + 1) * P], W2_flat[:, bass.ds(w2 + c * 2 * D, D)], start=False, stop=(c == FC - 1))
                last.then_inc(y_ps, 1)

            held = {}

            def step(turn, k):
                i = turn * RING + k
                if k == 0:
                    held.clear()
                if is_tile(i):
                    turn_rows(turn, k)
                if is_tile(i - 1):
                    if k - 1 not in held:
                        held[k - 1] = weights_of(i - 1)
                    first_product(i - 1, k - 1, held[k - 1])
                if is_tile(i) and k < RING - 1:
                    held[k] = weights_of(i)
                if is_tile(i - 3) and k - 3 not in held:
                    held[k - 3] = weights_of(i - 3)
                if is_tile(i - 2):
                    turn_hidden(i - 2, k)
                if is_tile(i - 3):
                    if isinstance(i, int) and i == 3:
                        pe.wait_ge(w2_lo, 1)
                    second_product(i - 3, k - 3, held[k - 3])

            each_tile(pe, NT + 3, step)


_INS = ['x', 'itok_B_6_14', 'L0_cond_ln_g', 'L0_cond_ln_b', 'L0_cond_subj_emb', 'L0_cond_hyp_w1', 'L0_cond_hyp_b1',
        'L0_cond_hyp_w2', 'L0_cond_hyp_b2', 'L0_cond_sty_w1', 'L0_cond_sty_b1', 'L0_cond_sty_w2', 'L0_cond_sty_b2',
        'L0_cond_router_w', 'L0_cond_exp_w1', 'L0_cond_exp_b1', 'L0_cond_exp_w2', 'L0_cond_exp_b2']


def kernel(**inputs):
    import numpy as _np
    import concourse.bacc as _bacc
    from concourse import mybir as _mybir
    from concourse.bass_utils import run_bass_kernel_spmd as _run

    nc = _bacc.Bacc("TRN2", target_bir_lowering=False, num_devices=1)
    arrays, args = {}, []
    for name in _INS:
        a = _np.ascontiguousarray(inputs[name])
        arrays[f"in_{name}_dram"] = a
        args.append(nc.dram_tensor(f"in_{name}_dram", a.shape, _mybir.dt.from_np(a.dtype), kind="ExternalInput").ap())
    args.append(nc.dram_tensor("out_0_dram", (B, T, D), _mybir.dt.float32, kind="ExternalOutput").ap())
    conditional_moe_kernel(nc, *args)
    r = _run(nc, [arrays], core_ids=[0])
    return r.results[0]["out_0_dram"]
```

```python
import concourse.bass as bass
from concourse import mybir
from contextlib import ExitStack

B, T, D = 128, 32, 128
E, FF = 8, 512
SE, SH, S2 = 64, 128, 64
P = 128
FC = FF // P
TOPK = 2
PHASE_T = 8
PHASES = T // PHASE_T
FIRST_PHASE = (0, 1, PHASES)
GROUPS = len(FIRST_PHASE) - 1
T0 = [p * PHASE_T for p in FIRST_PHASE]
LOAD_T = 8
CHUNK = 4
NCH = T // CHUNK
ROW = D + 2
TILES_BY = [TOPK * B * PHASE_T * (p + 1) // P - (E - 1) for p in range(PHASES)]
TILES_BY[-1] += 2 * (E - 1)
NT = TILES_BY[-1]
REGION = T * B + P
ZEROS_AT = E * REGION
TABLE_ROWS = ZEROS_AT + (E - 1) * P
AHEAD = 36
SPREAD = 25
H_DVE = 5
TURNED_AHEAD = 3
MEAN_PE, VAR_PE = 5, 5
NOWHERE = 1 << 20
RING = 16
EPS_LN, EPS_IN, EPS_SP = 1e-5, 1e-8, 1e-8
BIG = 1e30


def later(i, n):
    return i >= n if isinstance(i, int) else True


def is_tile(i):
    return 0 <= i < NT if isinstance(i, int) else True


def each_tile(eng, n_tiles, step):
    for k in range(RING):
        step(0, k)
    with eng.Fori(1, NT // RING, 1) as turn:
        for k in range(RING):
            step(turn, k)
    for i in range(NT // RING * RING, n_tiles):
        step(i // RING, i % RING)


def conditional_moe_kernel(nc, x, ids, ln_g, ln_b, subj_emb, hyp_w1, hyp_b1, hyp_w2, hyp_b2,
                           sty_w1, sty_b1, sty_w2, sty_b2, router_w, exp_w1, exp_b1, exp_w2, exp_b2, out):
    fp32, i32 = mybir.dt.float32, mybir.dt.int32
    ALU, ACT, AX = mybir.AluOpType, mybir.ActivationFunctionType, mybir.AxisListType

    ctx = ExitStack()
    with ctx:
        def sb(name, shape, dt=fp32):
            return ctx.enter_context(nc.sbuf_tensor(name, shape, dt))

        def sem(name):
            return ctx.enter_context(nc.semaphore(name))

        rows = nc.dram_tensor("rows", [TABLE_ROWS, ROW], fp32, kind="Internal").ap()
        results = nc.dram_tensor("results", [TOPK * B * T, D], fp32, kind="Internal").ap()

        X = sb("X", [P, T, D])
        Z = sb("Z", [P, T, D])
        Q = sb("Q", [P, T, D])
        H = sb("H", [P, T, ROW])
        W1 = sb("W1", [P, E * FF])
        W2 = sb("W2", [P, E * FC * D])
        b1raw = sb("b1raw", [E * FC, P])
        B1 = sb("B1", [P, E * FC])
        B2 = sb("B2", [P, E * D])
        ident = sb("ident", [P, P])
        lower = sb("lower", [P, P])
        ones = sb("ones", [P, (T - PHASE_T) * E])
        filling = sb("filling", [P, ROW])
        idx = sb("idx", [P, 1], i32)
        se = sb("se", [P, SE])
        seT = sb("seT", [SE, P])
        hyp1T = sb("hyp1T", [SH, P])
        hyp2T = sb("hyp2T", [SH, P])
        sty1T = sb("sty1T", [S2, P])
        w_hyp1 = sb("w_hyp1", [SE, SH])
        w_hyp2 = sb("w_hyp2", [SH, SH])
        w_sty1 = sb("w_sty1", [SH, S2])
        w_sty2 = sb("w_sty2", [S2, 2 * D])
        b_hyp1 = sb("b_hyp1", [SH, 1])
        b_hyp2 = sb("b_hyp2", [SH, 1])
        b_sty1 = sb("b_sty1", [S2, 1])
        b_sty2 = sb("b_sty2", [1, 2 * D])
        w_router = sb("w_router", [D, E])
        gB = sb("gB", [P, D])
        bB = sb("bB", [P, D])
        stats = sb("stats", [P, T, 6])
        st = sb("st", [P, 6, T])
        gam = sb("gam", [P, 4, D])
        co = sb("co", [P, 10, D])
        CO_A, CO_C = 8, 9
        mk = sb("mk", [P, TOPK, T * E])
        rt = sb("rt", [P, 6, T * E])
        rs = sb("rs", [P, 12, T])
        gate = sb("gate", [P, TOPK, T])
        tie = sb("tie", [P, E])
        tie_i = sb("tie_i", [P, E], i32)
        both = sb("both", [P, E * T])
        scan = sb("scan", [P, GROUPS + E * T])
        cnt = sb("cnt", [P, 4, PHASES * E])
        first = sb("first", [P, PHASES * E])
        first_i = sb("first_i", [P, PHASES * E], i32)
        come = sb("come", [P, PHASES + 1, E])
        place = sb("place", [P, TOPK, T], i32)
        whole_i = sb("whole_i", [P, 2, PHASES, E], i32)
        whole = sb("whole", [P, PHASES + 1, E])
        seg = sb("seg", [P, 3, PHASES * E])
        seg_end = sb("seg_end", [P, PHASES * E + 1])
        jump = sb("jump", [P, PHASES * E + 1])
        next_expert = sb("next_expert", [P, PHASES * E])
        passed = sb("passed", [P, PHASES * E])
        steps_by = sb("steps_by", [P, 2, PHASES * E])
        tile_no = sb("tile_no", [P, 2])
        at = sb("at", [P, 1])
        at_i = sb("at_i", [P, 1], i32)
        fill_f = sb("fill_f", [1, E])
        row_of = sb("row_of", [1, NT], i32)
        bias_of = sb("bias_of", [1, NT], i32)
        expert_of = sb("expert_of", [1, NT], i32)
        fill_at = sb("fill_at", [1, E], i32)
        tile_in = sb("tile_in", [P, RING, ROW])
        hT = sb("hT", [P, 2, P])
        w1_tile = sb("w1_tile", [P, 4, FF])
        w2_tile = sb("w2_tile", [P, 4, FC * D])
        hid = sb("hid", [P, 2, FC, P])
        y = sb("y", [P, RING, D])

        ps = ctx.enter_context(nc.psum_tensor("ps", [P, 8, 512], fp32))
        pSeT, pHyp1, pHyp2, pSty1 = ps[0:SE, 0, 0:P], ps[0:SH, 0, P:2 * P], ps[0:SH, 0, 2 * P:3 * P], ps[0:S2, 0, 3 * P:4 * P]
        pSty = ps[:, 1, 0:2 * D]
        pMean, pVar = ps[:, 2, :], ps[:, 3, :]
        pLogit = [ps[:, bank, 2 * D:2 * D + T * E] for bank in (2, 1)]
        pCount = ps[:, 0, 0:2 * PHASES * E]
        pList = ps[0:1, 0, 256:256 + 2 * NT]
        pHT = [ps[:, 4 + n, :] for n in range(4)]
        pHid = [ps[:, 2 * n:2 * n + 2, 0:2 * P].rearrange("p b (c r) -> p b c r", r=P) for n in range(2)]
        pB1 = ps[:, 0, P:P + E * FC]
        pTile, pY = [ps[:, 4 + n, 0:P] for n in range(2)], [ps[:, 6 + n, 0:D] for n in range(2)]

        x_in = [sem(f"x_in{c}") for c in range(T // LOAD_T)]
        ids_in, se_in, style_in, norm_in = sem("ids_in"), sem("se_in"), sem("style_in"), sem("norm_in")
        w1_in, w2_in, b1_in, b2_in = sem("w1_in"), sem("w2_in"), sem("b1_in"), sem("b2_in")
        ident_ready, consts = sem("ident_ready"), sem("consts")
        pool_step, dve_step, act_step = sem("pool_step"), sem("dve_step"), sem("act_step")
        seT_ps, seT_sb, hyp1_ps, hyp1_sb, hyp2_ps, hyp2_sb, sty1_ps, sty1_sb, sty_ps = (
            sem(n) for n in ("seT_ps", "seT_sb", "hyp1_ps", "hyp1_sb", "hyp2_ps", "hyp2_sb", "sty1_ps", "sty1_sb", "sty_ps"))
        gamma_ln = sem("gamma_ln")
        var_ready, sd_ready, rsd_ready, z_ready, z_act, mean_ps = (
            sem(n) for n in ("var_ready", "sd_ready", "rsd_ready", "z_ready", "z_act", "mean_ps"))
        zc_ready, sq_ready, var_ps, vt_ready, sdt_ready = (
            sem(n) for n in ("zc_ready", "sq_ready", "var_ps", "vt_ready", "sdt_ready"))
        norm_ready, h_ready, h_pool, hT_ps, hT_sb, logit_ps = (
            sem(n) for n in ("norm_ready", "h_ready", "h_pool", "hT_ps", "hT_sb", "logit_ps"))
        d_ready, exp_ready, runs_ready, count_ps = sem("d_ready"), sem("exp_ready"), sem("runs_ready"), sem("count_ps")
        second_ready = sem("second_ready")
        place_ready, gate_ready, fill_ready, list_ready, list_ps, tiles_ready = (
            sem(n) for n in ("place_ready", "gate_ready", "fill_ready", "list_ready", "list_ps", "tiles_ready"))
        b1_ps, b1_sb = sem("b1_ps"), sem("b1_sb")
        sent = [[sem(f"sent{c}_{k}") for k in range(TOPK)] for c in range(NCH)]
        filled = sem("filled")
        loaded = [sem(f"loaded{n}") for n in range(RING)]
        returned = [sem(f"returned{n}") for n in range(RING)]
        to_return = sem("to_return")
        tile_ps, tile_sb, hid_ps, hid_sb, y_ps, y_sum, y_sb = (
            sem(n) for n in ("tile_ps", "tile_sb", "hid_ps", "hid_sb", "y_ps", "y_sum", "y_sb"))
        weights_ready = sem("weights_ready")
        to_bias = sem("to_bias")
        back_in = [[sem(f"back{c}_{k}") for k in range(TOPK)] for c in range(NCH)]
        out_ready, out_done = sem("out_ready"), sem("out_done")

        block = ctx.enter_context(nc.Block())

        def tiles_left(n):
            return 16 * n

        res = results.rearrange("(k b t) d -> k b t d", k=TOPK, b=B)

        @block.sync
        def _(sp):
            for c in range(T // LOAD_T):
                t = slice(c * LOAD_T, (c + 1) * LOAD_T)
                sp.dma_start(X[:, t, :], x[:, t, :]).then_inc(x_in[c], 16)
            sp.dma_start(b_hyp1[:, :], hyp_b1.rearrange("(b a) -> b a", a=1)).then_inc(style_in, 16)
            sp.dma_start(b_hyp2[:, :], hyp_b2.rearrange("(b a) -> b a", a=1)).then_inc(style_in, 16)
            sp.dma_start(b_sty1[:, :], sty_b1.rearrange("(b a) -> b a", a=1)).then_inc(style_in, 16)
            sp.dma_start(b_sty2[:, :], sty_b2.rearrange("(a b) -> a b", a=1)).then_inc(style_in, 16)
            sp.dma_start(w_router[:, :], router_w).then_inc(norm_in, 16)
            sp.dma_start(gB[:, :], ln_g.rearrange("(a b) -> a b", a=1).to_broadcast([P, D])).then_inc(norm_in, 16)
            sp.dma_start(bB[:, :], ln_b.rearrange("(a b) -> a b", a=1).to_broadcast([P, D])).then_inc(norm_in, 16)
            sp.wait_ge(style_in, 16 * 8)
            sp.wait_ge(se_in, 16)
            sp.dma_start(W1[:, :].rearrange("d (e f) -> d e f", e=E), exp_w1.rearrange("e d f -> d e f")).then_inc(w1_in, 16)
            sp.dma_start(b1raw[:, :], exp_b1.rearrange("e (c p) -> (e c) p", p=P)).then_inc(b1_in, 16)
            sp.dma_start(B2[:, :], exp_b2.rearrange("(a e) d -> a (e d)", a=1).to_broadcast([P, E * D])).then_inc(b2_in, 16)
            sp.dma_start(W2[:, :].rearrange("p (n d) -> p n d", d=D), exp_w2.rearrange("e (c p) d -> p (e c) d", p=P)).then_inc(w2_in, 16)

            sp.wait_ge(consts, 1)
            sp.dma_start(rows[ZEROS_AT:TABLE_ROWS, :].rearrange("(n p) w -> p n w", p=P),
                         filling[:, :].rearrange("p (a w) -> p a w", a=1).to_broadcast([P, E - 1, ROW])).then_inc(filled, 16)

            def fill():
                sp.wait_ge(fill_ready, 1)
                for e in range(E):
                    r = sp.value_load(fill_at[0:1, e:e + 1], min_val=0, max_val=TABLE_ROWS - P)
                    sp.dma_start(rows[bass.ds(r, P), :], filling[:, :]).then_inc(filled, 16)

            def load(turn, k):
                i = turn * RING + k
                r = sp.value_load(row_of[0:1, bass.ds(i, 1)], min_val=0, max_val=TABLE_ROWS - P)
                if later(turn, 1):
                    sp.wait_ge(returned[k], tiles_left(turn))
                sp.dma_start(tile_in[:, k, :], rows[bass.ds(r, P), :]).then_inc(loaded[k], 16)

            def loads(first, last):
                lo, hi = max(-(-first // RING), 1), last // RING
                for i in range(first, min(lo * RING, last)):
                    load(i // RING, i % RING)
                if hi > lo:
                    with sp.Fori(lo, hi, 1) as turn:
                        for k in range(RING):
                            load(turn, k)
                for i in range(max(hi, lo) * RING, last):
                    load(i // RING, i % RING)

            for p in range(PHASES):
                sp.wait_ge(tiles_ready, 1 if p < FIRST_PHASE[1] else 2)
                for c in range(p * PHASE_T // CHUNK, (p + 1) * PHASE_T // CHUNK):
                    for k in range(TOPK):
                        sp.wait_ge(sent[c][k], 16 * CHUNK)
                if p == PHASES - 1:
                    sp.wait_ge(filled, 16 * (E + 1))
                loads(TILES_BY[p - 1] if p else 0, TILES_BY[p])
                if p == 0:
                    fill()

            for n in range(RING):
                sp.wait_ge(returned[n], tiles_left(len(range(n, NT, RING))))
            for c in range(NCH):
                t = slice(c * CHUNK, (c + 1) * CHUNK)
                sp.dma_start(Z[:, t, :], res[0][:, t, :]).then_inc(back_in[c][0], 16)
                sp.dma_start(Q[:, t, :], res[1][:, t, :]).then_inc(back_in[c][1], 16)
            for c in range(NCH):
                t = slice(c * CHUNK, (c + 1) * CHUNK)
                sp.wait_ge(out_ready, c + 1)
                sp.dma_start(out[:, t, :], X[:, t, :]).then_inc(out_done, 16)
            sp.wait_ge(out_done, 16 * NCH)

        @block.gpsimd
        def _(pool):
            steps = [0]

            def settle(ins):
                steps[0] += 1
                ins.then_inc(pool_step, 1)
                pool.wait_ge(pool_step, steps[0])

            settle(pool.memset(ident[:, :], 0.0))
            pool.affine_select(out=ident[:, :], in_=ident[:, :], compare_op=ALU.not_equal, fill=1.0,
                               base=0, pattern=[[-1, P]], channel_multiplier=1).then_inc(ident_ready, 1)
            pool.memset(ones[:, :], 1.0).then_inc(ident_ready, 1)
            pool.wait_ge(ids_in, 16)
            pool.indirect_dma_start(out=se[:, :], out_offset=None, in_=subj_emb[:, :],
                                    in_offset=bass.IndirectOffsetOnAxis(ap=idx[:, 0:1], axis=0)).then_inc(se_in, 16)
            pool.memset(lower[:, :], 1.0)
            pool.memset(scan[:, :], 0.0)
            settle(pool.memset(filling[:, :], 0.0))
            pool.iota(filling[:, D + 1:D + 2].bitcast(i32), [[0, 1]], base=NOWHERE, channel_multiplier=0)
            pool.affine_select(out=lower[:, :], in_=lower[:, :], compare_op=ALU.is_gt, fill=0.0,
                               base=0, pattern=[[1, P]], channel_multiplier=-1)
            pool.iota(at_i[:, :], [[0, 1]], base=0, channel_multiplier=P)
            pool.iota(first_i[:, :], [[0, PHASES], [REGION, E]], base=-1, channel_multiplier=0)
            pool.memset(come[:, :, :], 0.0)
            pool.memset(whole[:, :, :], 0.0)
            pool.memset(seg_end[:, :], 0.0)
            pool.memset(next_expert[:, :], 1.0)
            settle(pool.memset(passed[:, :], 0.0))
            for p in range(PHASES):
                pool.memset(next_expert[:, p * E + E - 1:p * E + E], float(1 - E) if p < PHASES - 1 else 0.0)
            settle(pool.iota(tie_i[:, :], [[-1, E]], base=E, channel_multiplier=0))
            pool.tensor_copy(at[:, :], at_i[:, :])
            pool.tensor_copy(first[:, :], first_i[:, :])
            pool.tensor_copy(tie[:, :], tie_i[:, :]).then_inc(consts, 1)

            settle(pool.iota(H[:, :, D + 1:D + 2].bitcast(i32), [[1, T], [0, 1]], base=0, channel_multiplier=T))

            pool.wait_ge(norm_ready, 1)
            for n in range(H_DVE, NCH):
                t = slice(4 * n, 4 * n + 4)
                over_t = lambda a: co[:, a:a + 1, :].to_broadcast([P, 4, D])
                settle(pool.tensor_tensor(H[:, t, 0:D], Z[:, t, :], over_t(CO_A), ALU.mult))
                pool.tensor_tensor(H[:, t, 0:D], H[:, t, 0:D], over_t(CO_C), ALU.add).then_inc(h_pool, 1)
            pool.wait_ge(h_pool, NCH - H_DVE)

            def send(t, k):
                pool.indirect_dma_start(out=rows[:, :], out_offset=bass.IndirectOffsetOnAxis(ap=place[:, k, t:t + 1], axis=0),
                                        in_=H[:, t, :], in_offset=None).then_inc(sent[t // CHUNK][k], 16)

            def turn_over(c):
                pool.wait_ge(sent[c][0], 16 * CHUNK)
                t = slice(c * CHUNK, (c + 1) * CHUNK)
                pool.iota(H[:, t, D + 1:D + 2].bitcast(i32), [[1, CHUNK], [0, 1]], base=B * T + c * CHUNK, channel_multiplier=T)
                settle(pool.tensor_copy(H[:, t, D:D + 1], gate[:, 1, t].rearrange("p (t a) -> p t a", a=1)))

            def sends(which):
                for s in which:
                    p, r = divmod(s, TOPK * PHASE_T)
                    k, t = r // PHASE_T, p * PHASE_T + r % PHASE_T
                    if r == 0 and p in FIRST_PHASE:
                        g = FIRST_PHASE.index(p)
                        pool.wait_ge(h_ready, min(T0[g + 1] // CHUNK, H_DVE))
                        pool.wait_ge(place_ready, 2 * g + 2)
                        pool.wait_ge(gate_ready, g + 1)
                    if k == 1 and t % CHUNK == 0:
                        turn_over(t // CHUNK)
                    send(t, k)

            limit = pool.to_reg(TOPK * B * T - 1)

            def give_back(turn, k):
                i = turn * RING + k
                pool.wait_ge(y_sb, i + 1)
                if not isinstance(i, int):
                    pool.sem_inc(to_return, 1)
                pool.indirect_dma_start(out=results[:, :],
                                        out_offset=bass.IndirectOffsetOnAxis(ap=tile_in[:, k, D + 1:D + 2].bitcast(i32), axis=0),
                                        in_=y[:, k, :], in_offset=None,
                                        bounds_check=limit, oob_is_err=False).then_inc(returned[k], 16)

            sends(range(AHEAD))
            left = TOPK * T - AHEAD
            looped = -(-SPREAD // RING)
            for i in range(looped * RING):
                give_back(i // RING, i % RING)
                done, now = (left * min(a, SPREAD) // SPREAD for a in (i, i + 1))
                sends(range(AHEAD + done, AHEAD + now))
            with pool.Fori(looped, NT // RING, 1) as turn:
                for k in range(RING):
                    give_back(turn, k)
            for i in range(NT // RING * RING, NT):
                give_back(i // RING, i % RING)

        @block.scalar
        def _(act):
            act.dma_start(idx[:, :], ids.rearrange("(b a) -> b a", a=1)).then_inc(ids_in, 16)
            act.dma_start(w_hyp1[:, :], hyp_w1).then_inc(style_in, 16)
            act.dma_start(w_hyp2[:, :], hyp_w2).then_inc(style_in, 16)
            act.dma_start(w_sty1[:, :], sty_w1).then_inc(style_in, 16)
            act.dma_start(w_sty2[:, :], sty_w2).then_inc(style_in, 16)

            def layer_sd(c):
                t = slice(c * LOAD_T, (c + 1) * LOAD_T)
                act.wait_ge(var_ready, c + 1)
                act.activation(st[:, 2, t], st[:, 1, t], ACT.Sqrt).then_inc(sd_ready, 1)

            def layer_norm(c):
                act.wait_ge(rsd_ready, c + 1)
                for t in range(c * LOAD_T + LOAD_T // 2, (c + 1) * LOAD_T):
                    last = act.activation(Z[:, t, :], X[:, t, :], ACT.Identity, scale=st[:, 3, t:t + 1], bias=st[:, 5, t:t + 1])
                last.then_inc(z_act, 1)

            layer_sd(0)
            act.wait_ge(style_in, 16 * 8)
            act.wait_ge(hyp1_ps, 1)
            act.activation(hyp1T[:, :], pHyp1, ACT.Relu, bias=b_hyp1[:, :]).then_inc(hyp1_sb, 1)
            layer_sd(1)
            layer_norm(0)
            act.wait_ge(hyp2_ps, 1)
            act.activation(hyp2T[:, :], pHyp2, ACT.Identity, bias=b_hyp2[:, :]).then_inc(hyp2_sb, 1)
            layer_sd(2)
            layer_norm(1)
            act.wait_ge(sty1_ps, 1)
            act.activation(sty1T[:, :], pSty1, ACT.Relu, bias=b_sty1[:, :]).then_inc(sty1_sb, 1)
            layer_sd(3)
            layer_norm(2)
            layer_norm(3)
            act.wait_ge(sty_ps, 1)
            act.activation(gam[:, 0, :], pSty[:, 0:D], ACT.Abs).then_inc(act_step, 1)
            act.wait_ge(act_step, 1)
            act.activation(gam[:, 1, :], gam[:, 0, :], ACT.Exp, scale=-1.0).then_inc(act_step, 1)
            act.wait_ge(act_step, 2)
            act.activation(gam[:, 2, :], gam[:, 1, :], ACT.Ln, bias=1.0).then_inc(gamma_ln, 1)
            for n in range(NCH):
                act.wait_ge(zc_ready, n + 1)
                act.activation(Q[:, 4 * n:4 * n + 4, :], Q[:, 4 * n:4 * n + 4, :], ACT.Square).then_inc(sq_ready, 1)
            act.wait_ge(vt_ready, 1)
            act.activation(co[:, 3, :], co[:, 2, :], ACT.Sqrt).then_inc(sdt_ready, 1)

            def turned_out(chunks):
                for n in chunks:
                    act.wait_ge(hT_ps, n + 1)
                    act.activation(Q[:, 4 * n:4 * n + 4, :], pHT[n % 4].rearrange("p (t d) -> p t d", d=P), ACT.Copy).then_inc(hT_sb, 1)

            def exponentials(g):
                te = slice(T0[g] * E, T0[g + 1] * E)
                t = slice(T0[g], T0[g + 1])
                act.wait_ge(d_ready, g + 1)
                act.activation(rt[:, 1, te], rt[:, 0, te], ACT.Exp)
                act.wait_ge(second_ready, g + 1)
                act.activation(rs[:, 8, t], rs[:, 2, t], ACT.Exp).then_inc(exp_ready, 1)

            act.wait_ge(var_ps, 1)
            act.wait_ge(vt_ready, 1)
            act.wait_ge(b1_ps, 1)
            act.activation(B1[:, :], pB1, ACT.Copy).then_inc(b1_sb, 1)
            turned_out(range(TURNED_AHEAD))
            exponentials(0)
            turned_out(range(TURNED_AHEAD, NCH))
            exponentials(1)
            act.wait_ge(tiles_ready, GROUPS)
            act.wait_ge(b1_sb, 1)

            def bias_at(i):
                return act.value_load(bias_of[0:1, bass.ds(i, 1)], min_val=0, max_val=(E - 1) * FC)

            ahead = {}

            def step(turn, k):
                i = turn * RING + k
                if is_tile(i - 1):
                    b = ahead.pop(k - 1, None) if k > 0 else None
                    if b is None:
                        b = bias_at(i - 1)
                    if later(i, 3):
                        act.wait_ge(y_ps, i - 2)
                    for c in range(FC):
                        if c % 2 == 0:
                            act.wait_ge(hid_ps, 2 * i - 1 + c // 2)
                            act.sem_inc(to_bias, 1)
                        last = act.activation(hid[:, (k - 1) % 2, c, :], pHid[(k - 1) % 2][:, c // 2, c % 2, :], ACT.Relu, bias=B1[:, bass.ds(b + c, 1)])
                    last.then_inc(hid_sb, 1)
                if is_tile(i) and k < RING - 1:
                    ahead[k] = bias_at(i)
                if is_tile(i - 3):
                    m = (k - 3) % RING
                    act.wait_ge(y_sum, i - 2)
                    act.activation(y[:, m, :], y[:, m, :], ACT.Copy, scale=tile_in[:, m, D:D + 1]).then_inc(y_sb, 1)

            each_tile(act, NT + 3, step)

        @block.vector
        def _(dve):
            steps = [0]

            def settle(ins):
                steps[0] += 1
                ins.then_inc(dve_step, 1)
                dve.wait_ge(dve_step, steps[0])

            def over_t(ap, n):
                return ap.rearrange("p (a d) -> p a d", a=1).to_broadcast([P, n, D])

            def over_e(ap, n):
                return ap.rearrange("p (t a) -> p t a", a=1).to_broadcast([P, n, E])

            V = nc.vector
            MEAN, VAR, SD, RSD, TMP, MRSD = range(6)

            def layer_stats(c):
                dve.wait_ge(x_in[c], 16)
                for t in range(c * LOAD_T, (c + 1) * LOAD_T):
                    last = V.bn_stats(stats[:, t, :], X[:, t, :])
                settle(last)
                t = slice(c * LOAD_T, (c + 1) * LOAD_T)
                me, mo, ve, vo = (stats[:, t, n] for n in (1, 4, 2, 5))
                V.tensor_tensor(st[:, MEAN, t], me, mo, ALU.add)
                V.tensor_tensor(st[:, VAR, t], ve, vo, ALU.add)
                settle(V.tensor_tensor(st[:, TMP, t], me, mo, ALU.subtract))
                V.tensor_scalar(st[:, MEAN, t], st[:, MEAN, t], 0.5, None, ALU.mult)
                V.tensor_scalar(st[:, VAR, t], st[:, VAR, t], 1.0 / D, EPS_LN, ALU.mult, ALU.add)
                settle(V.scalar_tensor_tensor(st[:, TMP, t], st[:, TMP, t], 0.25, st[:, TMP, t], ALU.mult, ALU.mult))
                V.tensor_tensor(st[:, VAR, t], st[:, VAR, t], st[:, TMP, t], ALU.add).then_inc(var_ready, 1)

            def layer_norm(c):
                t = slice(c * LOAD_T, (c + 1) * LOAD_T)
                dve.wait_ge(sd_ready, c + 1)
                settle(V.reciprocal(st[:, RSD, t], st[:, SD, t]))
                V.scalar_tensor_tensor(st[:, MRSD, t], st[:, MEAN, t], -1.0, st[:, RSD, t], ALU.mult, ALU.mult).then_inc(rsd_ready, 1)
                for t in range(c * LOAD_T, c * LOAD_T + LOAD_T // 2):
                    last = V.tensor_scalar(Z[:, t, :], X[:, t, :], st[:, MEAN, t:t + 1], st[:, RSD, t:t + 1], ALU.subtract, ALU.mult)
                last.then_inc(z_ready, 1)

            for c in range(T // LOAD_T + 1):
                if c < T // LOAD_T:
                    layer_stats(c)
                if c == 1:
                    dve.wait_ge(seT_ps, 1)
                    V.tensor_copy(seT[:, :], pSeT).then_inc(seT_sb, 1)
                if c >= 1:
                    layer_norm(c - 1)

            MZ, VZ, VT, SDT, RT, GG, MT, G2 = range(8)
            dve.wait_ge(norm_in, 16 * 3)
            V.tensor_tensor(co[:, G2, :], gB[:, :], gB[:, :], ALU.mult)
            dve.wait_ge(z_act, T // LOAD_T)
            dve.wait_ge(z_ready, T // LOAD_T)
            V.tensor_reduce(co[:, RT, :], Z[:, 4 * MEAN_PE:, :].rearrange("p t d -> p d t"), AX.X, ALU.add)
            dve.wait_ge(mean_ps, 1)
            settle(V.tensor_reduce(co[:, MZ, :], pMean.rearrange("p (t d) -> p d t", d=D), AX.X, ALU.add))
            settle(V.tensor_tensor(co[:, MZ, :], co[:, MZ, :], co[:, RT, :], ALU.add))
            settle(V.tensor_scalar(co[:, MZ, :], co[:, MZ, :], 1.0 / T, None, ALU.mult))
            for n in range(NCH):
                V.tensor_tensor(Q[:, 4 * n:4 * n + 4, :], Z[:, 4 * n:4 * n + 4, :], over_t(co[:, MZ, :], 4), ALU.subtract).then_inc(zc_ready, 1)
            dve.wait_ge(gamma_ln, 1)
            settle(V.scalar_tensor_tensor(gam[:, 3, :], pSty[:, 0:D], 0.0, gam[:, 2, :], ALU.max, ALU.add))
            settle(V.tensor_scalar(gam[:, 3, :], gam[:, 3, :], EPS_SP, None, ALU.add))
            V.tensor_tensor(co[:, GG, :], gB[:, :], gam[:, 3, :], ALU.mult)
            settle(V.tensor_tensor(co[:, MT, :], co[:, MZ, :], gB[:, :], ALU.mult))
            settle(V.tensor_tensor(co[:, MT, :], co[:, MT, :], bB[:, :], ALU.add))
            settle(V.tensor_tensor(co[:, MT, :], bB[:, :], co[:, MT, :], ALU.subtract))
            V.tensor_tensor(co[:, MT, :], co[:, MT, :], gam[:, 3, :], ALU.mult)
            dve.wait_ge(sq_ready, NCH)
            V.tensor_reduce(co[:, RT, :], Q[:, 4 * VAR_PE:, :].rearrange("p t d -> p d t"), AX.X, ALU.add)
            dve.wait_ge(var_ps, 1)
            settle(V.tensor_reduce(co[:, VZ, :], pVar.rearrange("p (t d) -> p d t", d=D), AX.X, ALU.add))
            settle(V.tensor_tensor(co[:, VZ, :], co[:, VZ, :], co[:, RT, :], ALU.add))
            settle(V.scalar_tensor_tensor(co[:, VT, :], co[:, VZ, :], 1.0 / T, co[:, G2, :], ALU.mult, ALU.mult))
            V.tensor_scalar(co[:, VT, :], co[:, VT, :], EPS_IN, None, ALU.add).then_inc(vt_ready, 1)
            dve.wait_ge(sdt_ready, 1)
            settle(V.reciprocal(co[:, RT, :], co[:, SDT, :]))
            V.tensor_tensor(co[:, CO_A, :], co[:, GG, :], co[:, RT, :], ALU.mult)
            settle(V.tensor_tensor(co[:, CO_C, :], co[:, MT, :], co[:, RT, :], ALU.mult))
            V.tensor_tensor(co[:, CO_C, :], co[:, CO_C, :], pSty[:, D:2 * D], ALU.add).then_inc(norm_ready, 1)
            dve.wait_ge(norm_ready, 1)

            def make_h(n):
                t = slice(4 * n, 4 * n + 4)
                settle(V.tensor_tensor(H[:, t, 0:D], Z[:, t, :], over_t(co[:, CO_A, :], 4), ALU.mult))
                V.tensor_tensor(H[:, t, 0:D], H[:, t, 0:D], over_t(co[:, CO_C, :], 4), ALU.add).then_inc(h_ready, 1)

            D0, EX, S0, D1, GE, S1 = range(6)

            def route(g):
                phases = range(FIRST_PHASE[g], FIRST_PHASE[g + 1])
                n, ts = T0[g + 1] - T0[g], slice(T0[g], T0[g + 1])
                cols = slice(T0[g] * E, T0[g + 1] * E)
                te = lambda ap: ap[:, cols].rearrange("p (t e) -> p t e", e=E)
                by_t = lambda ap: ap[:, cols].rearrange("p (s t e) -> p s t e", t=PHASE_T, e=E)
                by_e = lambda ap: ap[:, cols].rearrange("p (s e t) -> p s t e", t=PHASE_T, e=E)
                tie_bc = tie[:, :].rearrange("p (a e) -> p a e", a=1).to_broadcast([P, n, E])
                J = slice(phases[0] * E, (phases[-1] + 1) * E)
                logit = pLogit[g]
                dve.wait_ge(logit_ps, g + 1)
                settle(V.tensor_reduce(rs[:, 0, ts], te(logit), AX.X, ALU.max))
                V.tensor_tensor(te(rt[:, D0, :]), te(logit), over_e(rs[:, 0, ts], n), ALU.subtract).then_inc(d_ready, 1)
                dve.wait_ge(d_ready, g + 1)
                settle(V.scalar_tensor_tensor(te(rt[:, S0, :]), te(rt[:, D0, :]), 0.0, tie_bc, ALU.is_ge, ALU.mult))
                settle(V.tensor_reduce(rs[:, 1, ts], te(rt[:, S0, :]), AX.X, ALU.max))
                settle(V.tensor_tensor(te(mk[:, 0, :]), te(rt[:, S0, :]), over_e(rs[:, 1, ts], n), ALU.is_equal))
                settle(V.scalar_tensor_tensor(rt[:, D1, cols], mk[:, 0, cols], -BIG, rt[:, D0, cols], ALU.mult, ALU.add))
                V.tensor_reduce(rs[:, 2, ts], te(rt[:, D1, :]), AX.X, ALU.max).then_inc(second_ready, 1)
                dve.wait_ge(second_ready, g + 1)
                settle(V.tensor_tensor(te(rt[:, GE, :]), te(rt[:, D1, :]), over_e(rs[:, 2, ts], n), ALU.is_ge))
                settle(V.tensor_tensor(te(rt[:, GE, :]), te(rt[:, GE, :]), tie_bc, ALU.mult))
                settle(V.tensor_reduce(rs[:, 3, ts], te(rt[:, GE, :]), AX.X, ALU.max))
                settle(V.tensor_tensor(te(mk[:, 1, :]), te(rt[:, GE, :]), over_e(rs[:, 3, ts], n), ALU.is_equal))
                both_g = both[:, cols]
                s0 = g + T0[g] * E
                scan_g = scan[:, s0 + 1:s0 + 1 + n * E]
                settle(V.tensor_tensor(by_e(both), by_t(mk[:, 0, :]), by_t(mk[:, 1, :]), ALU.add))
                settle(V.tensor_tensor_scan(scan_g, ones[:, 0:n * E], both_g, 0.0, ALU.mult, ALU.add))
                s1 = s0 + n * E
                ends, starts = scan[:, s0 + PHASE_T:s1 + 1:PHASE_T], scan[:, s0:s1 - PHASE_T + 1:PHASE_T]
                V.tensor_tensor(cnt[:, 0, J], ends, starts, ALU.subtract).then_inc(runs_ready, 1)
                V.tensor_tensor(cnt[:, 1, J], first[:, J], starts, ALU.subtract)
                dve.wait_ge(exp_ready, g + 1)
                settle(V.tensor_reduce(rs[:, 4, ts], te(rt[:, EX, :]), AX.X, ALU.add))
                settle(V.reciprocal(rs[:, 5, ts], rs[:, 4, ts]))
                settle(V.tensor_tensor(rs[:, 6, ts], rs[:, 8, ts], rs[:, 5, ts], ALU.mult))
                settle(V.tensor_tensor(rs[:, 7, ts], rs[:, 5, ts], rs[:, 6, ts], ALU.add))
                dve.wait_ge(count_ps, g + 1)
                V.tensor_tensor(cnt[:, 2, J], cnt[:, 1, J], pCount[:, J], ALU.add)
                for p in phases:
                    settle(V.tensor_tensor(come[:, p + 1, :], come[:, p, :], pCount[:, (PHASES + p) * E:(PHASES + p + 1) * E], ALU.add))
                V.tensor_tensor(cnt[:, 3, J].rearrange("p (s e) -> p s e", e=E), cnt[:, 2, J].rearrange("p (s e) -> p s e", e=E),
                                come[:, phases[0]:phases[-1] + 1, :], ALU.add)
                settle(V.reciprocal(rs[:, 9, ts], rs[:, 7, ts]))
                V.tensor_tensor(gate[:, 1, ts], rs[:, 6, ts], rs[:, 9, ts], ALU.mult)
                V.tensor_tensor(H[:, ts, D], rs[:, 5, ts], rs[:, 9, ts], ALU.mult).then_inc(gate_ready, 1)
                settle(V.tensor_tensor(both_g.rearrange("p (j t) -> p j t", t=PHASE_T), scan_g.rearrange("p (j t) -> p j t", t=PHASE_T),
                                       cnt[:, 3, J].rearrange("p (j a) -> p j a", a=1).to_broadcast([P, len(phases) * E, PHASE_T]), ALU.add))
                V.tensor_tensor(by_t(rt[:, S0, :]), by_e(both), by_t(mk[:, 0, :]), ALU.mult)
                settle(V.tensor_tensor(by_t(rt[:, S1, :]), by_e(both), by_t(mk[:, 1, :]), ALU.mult))
                V.tensor_reduce(rs[:, 10, ts], te(rt[:, S0, :]), AX.X, ALU.add)
                settle(V.tensor_reduce(rs[:, 11, ts], te(rt[:, S1, :]), AX.X, ALU.add))
                V.tensor_copy(place[:, 0, ts], rs[:, 10, ts]).then_inc(place_ready, 1)
                V.tensor_copy(place[:, 1, ts], rs[:, 11, ts]).then_inc(place_ready, 1)

            def list_tiles(g):
                known = FIRST_PHASE[g + 1]
                J = slice(0, known * E)
                pe_ = lambda ap: ap.rearrange("p (s e) -> p s e", e=E)
                full = min(known, PHASES - 1)
                if known == PHASES:
                    settle(V.scalar_tensor_tensor(fill_f[:, :], first[0:1, 0:E], 1.0, come[0:1, PHASES, :], ALU.add, ALU.add))
                    V.tensor_copy(fill_at[:, :], fill_f[:, :]).then_inc(fill_ready, 1)
                    V.tensor_scalar(whole_i[:, 0, full, :], come[:, known, :], float(P - 1), None, ALU.add)
                settle(V.tensor_copy(whole_i[:, 0, 0:full, :], come[:, 1:full + 1, :]))
                settle(V.tensor_scalar(whole_i[:, 1, 0:known, :], whole_i[:, 0, 0:known, :], P.bit_length() - 1, P.bit_length() - 1,
                                       ALU.logical_shift_right, ALU.logical_shift_left))
                settle(V.tensor_copy(whole[:, 1:known + 1, :], whole_i[:, 1, 0:known, :]))
                V.tensor_tensor(pe_(seg[:, 1, J]), whole[:, 0:known, :], pe_(first[:, J]), ALU.add)
                settle(V.tensor_tensor(pe_(seg[:, 0, J]), whole[:, 1:known + 1, :], whole[:, 0:known, :], ALU.subtract))
                settle(V.tensor_tensor_scan(seg_end[:, 1:known * E + 1], ones[:, J], seg[:, 0, J], 0.0, ALU.mult, ALU.add))
                V.tensor_scalar(jump[:, known * E:known * E + 1], seg_end[:, known * E:known * E + 1], -1.0, float(ZEROS_AT - 1), ALU.mult, ALU.add)
                V.tensor_scalar(passed[:, J], seg_end[:, 1:known * E + 1], at[:, 0:1], None, ALU.is_le)
                settle(V.tensor_tensor(jump[:, J], seg[:, 1, J], seg_end[:, J], ALU.subtract))
                V.tensor_tensor(steps_by[:, 1, J], passed[:, J], next_expert[:, J], ALU.mult)
                settle(V.tensor_tensor(seg[:, 2, J], jump[:, 1:known * E + 1], jump[:, J], ALU.subtract))
                settle(V.tensor_tensor(steps_by[:, 0, J], passed[:, J], seg[:, 2, J], ALU.mult))
                settle(V.tensor_reduce(tile_no[:, :], steps_by[:, :, J], AX.X, ALU.add))
                V.tensor_tensor(tile_no[:, 0:1], tile_no[:, 0:1], at[:, :], ALU.add).then_inc(list_ready, 1)

            def tiles_out(g):
                tiles = slice(0, TILES_BY[0]) if g == 0 else slice(TILES_BY[0], NT)
                dve.wait_ge(list_ps, g + 1)
                row, expert = pList[:, 0:NT], pList[:, NT:2 * NT]
                V.tensor_scalar(bias_of[:, tiles], expert[:, tiles], float(FC), None, ALU.mult)
                V.tensor_scalar(expert_of[:, tiles], expert[:, tiles], float(FF), None, ALU.mult)
                V.tensor_copy(row_of[:, tiles], row[:, tiles]).then_inc(tiles_ready, 1)
                dve.wait_ge(tiles_ready, g + 1)

            dve.wait_ge(consts, 1)
            for n in range(H_DVE):
                make_h(n)
            route(0)
            list_tiles(0)
            tiles_out(0)
            route(1)
            list_tiles(1)
            tiles_out(1)
            dve.wait_ge(w1_in, 16)
            dve.wait_ge(w2_in, 16)
            dve.wait_ge(b2_in, 16)

            def weights(i, k):
                w = dve.value_load(expert_of[0:1, bass.ds(i, 1)], min_val=0, max_val=(E - 1) * FF)
                V.tensor_copy(w1_tile[:, k % 4, :], W1[:, bass.ds(w, FF)])
                V.tensor_copy(w2_tile[:, k % 4, :], W2[:, bass.ds(w, FC * D)]).then_inc(weights_ready, 1)
                return w

            kept = {}

            def step(turn, k):
                i = turn * RING + k
                if k == 0:
                    kept.clear()
                if is_tile(i):
                    dve.wait_ge(tile_ps, i + 1)
                    if later(i, 2):
                        dve.wait_ge(hid_ps, 2 * i - 2)
                    V.tensor_copy(hT[:, k % 2, :], pTile[k % 2]).then_inc(tile_sb, 1)
                if is_tile(i + 1):
                    kept[k + 1] = weights(i + 1, k + 1)
                if is_tile(i - 2):
                    m = (k - 2) % RING
                    w = kept.pop(k - 2, None)
                    if w is None:
                        w = dve.value_load(expert_of[0:1, bass.ds(i - 2, 1)], min_val=0, max_val=(E - 1) * FF)
                    dve.wait_ge(y_ps, i - 1)
                    V.tensor_tensor(y[:, m, :], pY[m % 2], B2[:, bass.ds(w // FC, D)], ALU.add).then_inc(y_sum, 1)

            weights(0, 0)
            each_tile(dve, NT + 2, step)

            for c in range(NCH):
                t = slice(c * CHUNK, (c + 1) * CHUNK)
                dve.wait_ge(back_in[c][0], 16)
                dve.wait_ge(back_in[c][1], 16)
                settle(V.tensor_tensor(Z[:, t, :], Z[:, t, :], Q[:, t, :], ALU.add))
                V.tensor_tensor(X[:, t, :], X[:, t, :], Z[:, t, :], ALU.add).then_inc(out_ready, 1)

        @block.tensor
        def _(pe):
            mm = nc.tensor.matmul
            pe.wait_ge(ident_ready, 2)
            pe.wait_ge(se_in, 16)
            nc.tensor.transpose(pSeT, se[:, :], ident[:, :]).then_inc(seT_ps, 1)
            pe.wait_ge(style_in, 16 * 8)
            pe.wait_ge(seT_sb, 1)
            mm(pHyp1, w_hyp1[:, :], seT[:, :], start=True, stop=True).then_inc(hyp1_ps, 1)
            def sum_z(n):
                pe.wait_ge(z_act if n % 2 else z_ready, n // 2 + 1)
                return mm(pMean, ident[:, :], Z[:, 4 * n:4 * n + 4, :].rearrange("p t d -> p (t d)"), start=(n == 0), stop=(n == MEAN_PE - 1))

            pe.wait_ge(hyp1_sb, 1)
            mm(pHyp2, w_hyp2[:, :], hyp1T[:, :], start=True, stop=True).then_inc(hyp2_ps, 1)
            sum_z(0)
            pe.wait_ge(hyp2_sb, 1)
            mm(pSty1, w_sty1[:, :], hyp2T[:, :], start=True, stop=True).then_inc(sty1_ps, 1)
            for n in range(1, MEAN_PE):
                last = sum_z(n)
            last.then_inc(mean_ps, 1)
            pe.wait_ge(sty1_sb, 1)
            mm(pSty, sty1T[:, :], w_sty2[:, :], start=True, stop=False)
            mm(pSty, ones[0:1, 0:P], b_sty2[:, :], start=False, stop=True).then_inc(sty_ps, 1)
            for n in range(VAR_PE):
                pe.wait_ge(sq_ready, n + 1)
                last = mm(pVar, ident[:, :], Q[:, 4 * n:4 * n + 4, :].rearrange("p t d -> p (t d)"), start=(n == 0), stop=(n == VAR_PE - 1))
            last.then_inc(var_ps, 1)

            pe.wait_ge(b1_in, 16)
            nc.tensor.transpose(pB1, b1raw[:, :], ident[0:E * FC, 0:E * FC]).then_inc(b1_ps, 1)

            def turn_h(n):
                if n < H_DVE:
                    pe.wait_ge(h_ready, n + 1)
                else:
                    pe.wait_ge(h_pool, n + 1 - H_DVE)
                if n >= 4:
                    pe.wait_ge(hT_sb, n - 3)
                for a in range(4):
                    last = nc.tensor.transpose(pHT[n % 4][:, a * P:(a + 1) * P], H[:, 4 * n + a, 0:D], ident[:, :])
                last.then_inc(hT_ps, 1)

            def logits(n):
                pe.wait_ge(hT_sb, n + 1)
                for t in range(4 * n, 4 * n + 4):
                    last = mm(pLogit[0 if t < T0[1] else 1][:, t * E:(t + 1) * E], Q[:, t, :], w_router[:, :], start=True, stop=True)
                return last

            pe.wait_ge(consts, 1)
            pe.wait_ge(b1_sb, 1)

            def counts(g):
                J = slice(FIRST_PHASE[g] * E, FIRST_PHASE[g + 1] * E)
                pe.wait_ge(runs_ready, g + 1)
                mm(pCount[:, J], lower[:, :], cnt[:, 0, J], start=True, stop=True)
                mm(pCount[:, PHASES * E + J.start:PHASES * E + J.stop], ones[:, 0:P], cnt[:, 0, J],
                   start=True, stop=True).then_inc(count_ps, 1)

            def list_turned(g):
                pe.wait_ge(list_ready, g + 1)
                for a in range(2):
                    last = mm(pList[:, a * NT:(a + 1) * NT], tile_no[:, a:a + 1], ident[:, 0:NT], start=True, stop=True)
                last.then_inc(list_ps, 1)

            pe.wait_ge(norm_in, 16 * 3)
            for n in range(NCH):
                if n == T0[1] // CHUNK:
                    logits(n - 1).then_inc(logit_ps, 1)
                    turn_h(n)
                else:
                    turn_h(n)
                    if n >= 1:
                        logits(n - 1)
                if n == TURNED_AHEAD:
                    counts(0)
                if n == NCH - 1:
                    list_turned(0)
            logits(NCH - 1).then_inc(logit_ps, 1)
            counts(1)
            list_turned(1)

            pe.wait_ge(tiles_ready, GROUPS)
            pe.wait_ge(hT_sb, NCH)

            def turn_rows(turn, k):
                i = turn * RING + k
                if later(i, 2):
                    pe.wait_ge(tile_sb, i - 1)
                pe.wait_ge(loaded[k], 16 * (turn + 1))
                nc.tensor.transpose(pTile[k % 2], tile_in[:, k, 0:D], ident[:, :]).then_inc(tile_ps, 1)

            def first_product(i, k):
                if later(i, 2):
                    pe.wait_ge(hid_sb, i - 1)
                pe.wait_ge(weights_ready, i + 1)
                pe.wait_ge(tile_sb, i + 1)
                for c in range(FC):
                    last = mm(pHid[k % 2][:, c // 2, c % 2, :], w1_tile[:, k % 4, c * P:(c + 1) * P], hT[:, k % 2, :], start=True, stop=True)
                    if c % 2 == 1:
                        last.then_inc(hid_ps, 1)

            def second_product(i, k):
                if later(i, 2):
                    pe.wait_ge(y_sum, i - 1)
                pe.wait_ge(hid_sb, i + 1)
                for c in range(FC):
                    last = mm(pY[k % 2], hid[:, k % 2, c, :], w2_tile[:, k % 4, c * D:(c + 1) * D], start=(c == 0), stop=(c == FC - 1))
                last.then_inc(y_ps, 1)

            def step(turn, k):
                i = turn * RING + k
                if is_tile(i):
                    turn_rows(turn, k)
                if is_tile(i - 1):
                    first_product(i - 1, (k - 1) % RING)
                if is_tile(i - 2):
                    second_product(i - 2, (k - 2) % RING)

            each_tile(pe, NT + 2, step)


_INS = ['x', 'itok_B_6_14', 'L0_cond_ln_g', 'L0_cond_ln_b', 'L0_cond_subj_emb', 'L0_cond_hyp_w1', 'L0_cond_hyp_b1',
        'L0_cond_hyp_w2', 'L0_cond_hyp_b2', 'L0_cond_sty_w1', 'L0_cond_sty_b1', 'L0_cond_sty_w2', 'L0_cond_sty_b2',
        'L0_cond_router_w', 'L0_cond_exp_w1', 'L0_cond_exp_b1', 'L0_cond_exp_w2', 'L0_cond_exp_b2']


def kernel(**inputs):
    import numpy as _np
    import concourse.bacc as _bacc
    from concourse import mybir as _mybir
    from concourse.bass_utils import run_bass_kernel_spmd as _run

    nc = _bacc.Bacc("TRN2", target_bir_lowering=False, num_devices=1)
    arrays, args = {}, []
    for name in _INS:
        a = _np.ascontiguousarray(inputs[name])
        arrays[f"in_{name}_dram"] = a
        args.append(nc.dram_tensor(f"in_{name}_dram", a.shape, _mybir.dt.from_np(a.dtype), kind="ExternalInput").ap())
    args.append(nc.dram_tensor("out_0_dram", (B, T, D), _mybir.dt.float32, kind="ExternalOutput").ap())
    conditional_moe_kernel(nc, *args)
    r = _run(nc, [arrays], core_ids=[0])
    return r.results[0]["out_0_dram"]
```
